# Optimizing a Trainium2 kernel written in Bass

```python
import numpy as np
import jax
import jax.numpy as jnp

def _softmax(x, axis=-1):
    return jax.nn.softmax(x, axis=axis)

def _gelu(x):
    return jax.nn.gelu(x, approximate=True)

def _silu(x):
    return jax.nn.silu(x)

def _sigmoid(x):
    return jax.nn.sigmoid(x)

def _layernorm(x, axis=-1, eps=1e-05):
    m = jnp.mean(x, axis=axis, keepdims=True)
    v = jnp.var(x, axis=axis, keepdims=True)
    return (x - m) / jnp.sqrt(v + eps)

def _scatter_add(tgt, idx, src, axis=0):
    return tgt.at[idx].add(src)

def _segment_sum(src, seg, n):
    return jax.ops.segment_sum(src, seg, n)
kernel_name = 'mk_audio_tower_d1_tok_audfeat512_r4_606d0a'

def setup_inputs(seed: int=0):
    np.random.seed(seed)
    _w = jnp.asarray

    def _rec_inputs():
        import jax
        import jax.numpy as jnp
        _rk = jax.random.key(seed)
        x = -3.53888e-05 + 1.00021 * jax.random.normal(jax.random.fold_in(_rk, 1), (16, 750, 23), jnp.float32)
        return x
    x = _rec_inputs()

    def _L0_tok_setup():
        import jax, jax.numpy as jnp
        import numpy as np
        CONTEXT = 5
        DILATION = 1
        BN_EPS = 1e-05

        def _tdnn_forward(x, W, b, gamma, beta):
            B, T, D = x.shape
            L = T - (CONTEXT - 1) * DILATION
            frames = jnp.stack([jax.lax.dynamic_slice_in_dim(x, k * DILATION, L, axis=1) for k in range(CONTEXT)], axis=2)
            patches = frames.reshape(B, L, CONTEXT * D)
            y = jnp.einsum('blf,of->blo', patches, W) + b
            y = jax.nn.relu(y)
            mean = jnp.mean(y, axis=(0, 1))
            var = jnp.var(y, axis=(0, 1))
            y = (y - mean) * jax.lax.rsqrt(var + BN_EPS) * gamma + beta
            return y
        key = jax.random.key(seed)
        k1, k2, k3 = jax.random.split(key, 3)
        B, T, D, O = (64, 1024, 23, 128)
        x = jax.random.normal(k1, (B, T, D), dtype=jnp.float32)
        fan_in = D * CONTEXT
        bound = 1.0 / np.sqrt(fan_in)
        W = jax.random.uniform(k2, (O, fan_in), dtype=jnp.float32, minval=-bound, maxval=bound)
        b = jax.random.uniform(k3, (O,), dtype=jnp.float32, minval=-bound, maxval=bound)
        gamma = jnp.ones((O,), dtype=jnp.float32)
        beta = jnp.zeros((O,), dtype=jnp.float32)
        return {'x': x, 'W': W, 'b': b, 'gamma': gamma, 'beta': beta}
    _L0_tok_all = _L0_tok_setup()
    _L0_tok_in = {k: v for k, v in _L0_tok_all.items() if k in ('W', 'b', 'gamma', 'beta')}
    del _L0_tok_all

    def _L0_attn_setup():
        import jax, jax.numpy as jnp
        import numpy as np
        N_HEAD = 8

        def _split_heads(x, n_head):
            b, s, c = x.shape
            return x.reshape(b, s, n_head, c // n_head).transpose(0, 2, 1, 3)
        key = jax.random.key(seed)
        ks = jax.random.split(key, 5)
        D = 128
        q = jax.random.normal(ks[0], (2, 1024, D), dtype=jnp.float32)
        s = 0.02
        Wq = jax.random.normal(ks[1], (D, D), dtype=jnp.float32) * s
        Wk = jax.random.normal(ks[2], (D, D), dtype=jnp.float32) * s
        Wv = jax.random.normal(ks[3], (D, D), dtype=jnp.float32) * s
        Wo = jax.random.normal(ks[4], (D, D), dtype=jnp.float32) * s
        z = jnp.zeros((D,), dtype=jnp.float32)
        return {'q': q, 'Wq': Wq, 'bq': z, 'Wk': Wk, 'bk': z, 'Wv': Wv, 'bv': z, 'Wo': Wo, 'bo': z}
    _L0_attn_all = _L0_attn_setup()
    _L0_attn_in = {k: v for k, v in _L0_attn_all.items() if k in ('Wq', 'bq', 'Wk', 'bk', 'Wv', 'bv', 'Wo', 'bo')}
    del _L0_attn_all

    def _L0_ffn_setup():
        import jax, jax.numpy as jnp
        import numpy as np
        B, S, D = (8, 1024, 128)
        H = 512
        O = 128
        E = 8
        TOP_K = 1
        key = jax.random.key(seed)
        ks = jax.random.split(key, 8)
        sc = 0.02
        return {'x': jax.random.normal(ks[0], (B, S, D), dtype=jnp.float32), 'Wr': jax.random.normal(ks[1], (D, E), dtype=jnp.float32) * sc, 'br': jnp.zeros((E,), dtype=jnp.float32), 'W1': jax.random.normal(ks[2], (E, D, H), dtype=jnp.float32) * sc, 'b1': jnp.zeros((E, H), dtype=jnp.float32), 'W2': jax.random.normal(ks[3], (E, H, O), dtype=jnp.float32) * sc, 'b2': jnp.zeros((E, O), dtype=jnp.float32)}
    _L0_ffn_all = _L0_ffn_setup()
    _L0_ffn_in = {k: v for k, v in _L0_ffn_all.items() if k in ('Wr', 'br', 'W1', 'b1', 'W2', 'b2')}
    del _L0_ffn_all
    return {'x': x, 'L0_tok_W': _L0_tok_in['W'], 'L0_tok_b': _L0_tok_in['b'], 'L0_tok_gamma': _L0_tok_in['gamma'], 'L0_tok_beta': _L0_tok_in['beta'], 'L0_attn_Wq': _L0_attn_in['Wq'], 'L0_attn_bq': _L0_attn_in['bq'], 'L0_attn_Wk': _L0_attn_in['Wk'], 'L0_attn_bk': _L0_attn_in['bk'], 'L0_attn_Wv': _L0_attn_in['Wv'], 'L0_attn_bv': _L0_attn_in['bv'], 'L0_attn_Wo': _L0_attn_in['Wo'], 'L0_attn_bo': _L0_attn_in['bo'], 'L0_ffn_Wr': _L0_ffn_in['Wr'], 'L0_ffn_br': _L0_ffn_in['br'], 'L0_ffn_W1': _L0_ffn_in['W1'], 'L0_ffn_b1': _L0_ffn_in['b1'], 'L0_ffn_W2': _L0_ffn_in['W2'], 'L0_ffn_b2': _L0_ffn_in['b2']}

def reference(x, L0_tok_W, L0_tok_b, L0_tok_gamma, L0_tok_beta, L0_attn_Wq, L0_attn_bq, L0_attn_Wk, L0_attn_bk, L0_attn_Wv, L0_attn_bv, L0_attn_Wo, L0_attn_bo, L0_ffn_Wr, L0_ffn_br, L0_ffn_W1, L0_ffn_b1, L0_ffn_W2, L0_ffn_b2):
    import jax
    import jax.numpy as jnp

    def _L0_tok_ref(x, W, b, gamma, beta):
        import jax, jax.numpy as jnp
        import numpy as np
        CONTEXT = 5
        DILATION = 1
        BN_EPS = 1e-05

        def _tdnn_forward(x, W, b, gamma, beta):
            B, T, D = x.shape
            L = T - (CONTEXT - 1) * DILATION
            frames = jnp.stack([jax.lax.dynamic_slice_in_dim(x, k * DILATION, L, axis=1) for k in range(CONTEXT)], axis=2)
            patches = frames.reshape(B, L, CONTEXT * D)
            y = jnp.einsum('blf,of->blo', patches, W) + b
            y = jax.nn.relu(y)
            mean = jnp.mean(y, axis=(0, 1))
            var = jnp.var(y, axis=(0, 1))
            y = (y - mean) * jax.lax.rsqrt(var + BN_EPS) * gamma + beta
            return y
        return _tdnn_forward(x, W, b, gamma, beta)

    def _L0_attn_ref(q, Wq, bq, Wk, bk, Wv, bv, Wo, bo):
        import jax, jax.numpy as jnp
        import numpy as np
        N_HEAD = 8

        def _split_heads(x, n_head):
            b, s, c = x.shape
            return x.reshape(b, s, n_head, c // n_head).transpose(0, 2, 1, 3)
        qp = _split_heads(q @ Wq.T + bq, N_HEAD)
        kp = _split_heads(q @ Wk.T + bk, N_HEAD)
        vp = _split_heads(q @ Wv.T + bv, N_HEAD)
        dh = qp.shape[-1]
        scale = 1.0 / jnp.sqrt(jnp.asarray(dh, dtype=qp.dtype))
        scores = jnp.einsum('bhqd,bhkd->bhqk', qp, kp) * scale
        probs = jax.nn.softmax(scores, axis=-1)
        attn = jnp.einsum('bhqk,bhkd->bhqd', probs, vp)
        b, h, s, _ = attn.shape
        merged = attn.transpose(0, 2, 1, 3).reshape(b, s, h * dh)
        return merged @ Wo.T + bo

    def _L0_ffn_ref(x, Wr, br, W1, b1, W2, b2):
        import jax, jax.numpy as jnp
        import numpy as np
        B, S, D = (8, 1024, 128)
        H = 512
        O = 128
        E = 8
        TOP_K = 1
        b, s, d = x.shape
        xf = x.reshape(-1, d)
        router_logits = xf @ Wr + br
        topk_logits, topk_idx = jax.lax.top_k(router_logits, TOP_K)
        topk_gates = jax.nn.softmax(topk_logits, axis=1)
        out = jnp.zeros((xf.shape[0], O), dtype=x.dtype)
        for k in range(TOP_K):
            idx_k = topk_idx[:, k]
            gate_k = topk_gates[:, k:k + 1]
            for e in range(E):
                h = jax.nn.relu(xf @ W1[e] + b1[e])
                oe = h @ W2[e] + b2[e]
                mask = (idx_k == e)[:, None]
                out = out + jnp.where(mask, gate_k * oe, 0.0)
        return out.reshape(b, s, O)
    h = _L0_tok_ref(x, L0_tok_W, L0_tok_b, L0_tok_gamma, L0_tok_beta)
    h = h + _L0_attn_ref(_layernorm(h, axis=-1), L0_attn_Wq, L0_attn_bq, L0_attn_Wk, L0_attn_bk, L0_attn_Wv, L0_attn_bv, L0_attn_Wo, L0_attn_bo)
    h = h + _L0_ffn_ref(_layernorm(h, axis=-1), L0_ffn_Wr, L0_ffn_br, L0_ffn_W1, L0_ffn_b1, L0_ffn_W2, L0_ffn_b2)
    return h

_drawn_inputs = setup_inputs


def setup_inputs(seed=0):
    import zlib

    import numpy as np

    out = dict(_drawn_inputs(seed))
    spreads = {'L0_tok_gamma': (1.0, 0.2),
     'L0_tok_beta': (0.0, 0.1),
     'L0_attn_bq': (0.0, 0.8),
     'L0_attn_bk': (0.0, 0.8),
     'L0_attn_bv': (0.0, 0.342),
     'L0_attn_bo': (0.0, 0.1),
     'L0_ffn_br': (0.0, 0.1),
     'L0_ffn_b1': (0.0, 0.285),
     'L0_ffn_b2': (0.0, 0.1)}
    factors = {'L0_attn_Wq': 8.0, 'L0_attn_Wk': 8.0, 'L0_attn_Wv': 6.776}
    for name, (base, spread) in spreads.items():
        noise = np.random.default_rng([zlib.crc32(name.encode()), seed]).standard_normal(out[name].shape)
        drawn = base * np.exp(spread * noise) if base else spread * noise
        out[name] = jnp.asarray(drawn.astype(out[name].dtype))
    for name, factor in factors.items():
        out[name] = (out[name] * factor).astype(out[name].dtype)
    return out
```

```python
import concourse.bass as bass
from concourse import mybir
from contextlib import ExitStack


def audio_tower(
    nc: bass.Bass,
    x_t: bass.AP,
    tok_w: bass.AP,
    tok_b: bass.AP,
    gamma: bass.AP,
    beta: bass.AP,
    wq: bass.AP,
    bq: bass.AP,
    wk: bass.AP,
    bk: bass.AP,
    wv: bass.AP,
    bv: bass.AP,
    wo: bass.AP,
    bo: bass.AP,
    wr: bass.AP,
    br: bass.AP,
    w1: bass.AP,
    b1: bass.AP,
    w2: bass.AP,
    b2: bass.AP,
    out: bass.AP,
):
    fp32 = mybir.dt.float32
    bf16 = mybir.dt.bfloat16
    i32 = mybir.dt.int32
    ALU = mybir.AluOpType
    ACT = mybir.ActivationFunctionType
    AX = mybir.AxisListType

    FEAT, B, T = x_t.shape
    TAPS, D = tok_w.shape
    CONTEXT = TAPS // FEAT
    L = T - CONTEXT + 1
    HALF = L // 2
    H = 8
    DH = D // H
    NT = -(-L // D)
    LP = NT * D
    LAST = L - (NT - 1) * D
    GH = 4
    E, _, HID = w1.shape
    JH = HID // D
    EPS = 1e-5
    SCALE = DH ** -0.5
    NTOK = B * L
    CAP = (-(-NTOK // D) + 1) * D
    DEAD = E * CAP
    SLOTS = (NTOK + E * (D - 1)) // D + 1
    FAR = 1 << 20
    ROW = 2 * D + 4
    ID, GATE = 2 * D, 2 * D + 1
    Q_PARTS = (0, 0, 1, 1, 0, 2)
    K_PARTS = (0, 1, 0, 1, 2, 0)
    KR = len(Q_PARTS) * DH
    KM = KR + 2
    STEPS = H * 2 * NT
    PASS = NT * GH
    GROUPS = STEPS // GH
    N_ST, N_MX, N_P = 3, 2, 3
    CH = 2
    NCH = B // CH

    q_dram = nc.dram_tensor("q_parts_dram", (D, 3, L), bf16).ap()
    k_dram = nc.dram_tensor("k_parts_dram", (D, 3, L), bf16).ap()
    rows_dram = nc.dram_tensor("routed_rows_dram", (DEAD + D, ROW), fp32).ap()
    out_rows = out.rearrange("b t d -> (b t) d")

    ctx = ExitStack()
    with ctx:
        def sb(name, shape, dt=fp32):
            return ctx.enter_context(nc.sbuf_tensor(name, shape, dt))

        def sem(name):
            return ctx.enter_context(nc.semaphore(name))

        seq = sb("seq", [128, B * LP])
        p_ring = sb("p_ring", [128, N_P * GH * HALF])
        patches = p_ring[0:TAPS, 0:N_P * CH * L].rearrange("p (n c t) -> p n c t", n=N_P, c=CH)
        probs = p_ring[:, :].rearrange("p (n j t) -> p n j t", n=N_P, j=GH)
        q_rows = [sb(f"q_rows{n}", [KM, H, LP], bf16) for n in range(2)]
        k_rows = [sb(f"k_rows{n}", [KM, H, L], bf16) for n in range(2)]
        values = [sb(f"values{n}", [128, NT, H, 32]) for n in range(2)]
        q_full, k_full = sb("q_full", [128, L]), sb("k_full", [128, L])
        q_rest, k_rest = sb("q_rest", [128, L]), sb("k_rest", [128, L])
        q_part, k_part = sb("q_part", [128, 3, L], bf16), sb("k_part", [128, 3, L], bf16)
        h_t = sb("h_t", [128, LP])
        h_cur = sb("h_cur", [128, NT, D])
        xn = sb("xn", [128, NT, D])
        xn_t = sb("xn_t", [128, LP])
        o_un = sb("o_un", [128, 2, LP])
        merged = sb("merged", [128, NT, D])
        merged_t = sb("merged_t", [128, LP])
        xn2_t = merged_t
        rows = sb("rows", [128, NT, ROW])
        half_max = sb("half_max", [128, STEPS])
        neg_max = sb("neg_max", [128, STEPS // 2])
        max_parts = sb("max_parts", [128, 2, NT, 2, GH], bf16)
        max_rows = [sb(f"max_rows{g}", [2 * GH, L], bf16) for g in range(2)]
        stats = sb("stats", [128, NT, 6])
        mv = sb("mv", [128, NT, 2])
        var_eps = sb("var_eps", [128, NT])
        rstd = sb("rstd", [128, NT])
        stats2 = sb("stats2", [128, NT, 6])
        mv2 = sb("mv2", [128, NT, 2])
        var_eps2 = sb("var_eps2", [128, NT])
        rstd2 = sb("rstd2", [128, NT])
        r_den = sb("r_den", [128, NT // 2 * H])
        logits = sb("logits", [128, NT, E])
        top = sb("top", [128, NT])
        scored = sb("scored", [128, NT, E])
        scored2 = sb("scored2", [128, NT, E])
        best = sb("best", [128, NT])
        picked = sb("picked", [128, NT, E])
        onehot = sb("onehot", [128, NT, E], bf16)
        g_diff = sb("g_diff", [128, NT])
        g_exp = sb("g_exp", [128, NT])
        g_inv = sb("g_inv", [128, NT])
        place = sb("place", [128, NT, E])
        place1 = sb("place1", [128, NT, E])
        pos = sb("pos", [128, NT])
        pos_i = sb("pos_i", [128, NT], i32)
        next_row = sb("next_row", [128, E])
        tok_id = sb("tok_id", [128, NT])
        tok_w_sb = sb("tok_w_sb", [TAPS, D])
        wq_sb, wk_sb, wv_sb, wo_sb = (sb(n, [128, D]) for n in ("wq_sb", "wk_sb", "wv_sb", "wo_sb"))
        wr_sb = sb("wr_sb", [128, E])
        tok_b_sb, gamma_sb, beta_sb, bq_sb, bk_sb, bq4 = (
            sb(n, [128, 1]) for n in ("tok_b_sb", "gamma_sb", "beta_sb", "bq_sb", "bk_sb", "bq4"))
        bv_bc, bo_bc, br_bc = sb("bv_bc", [128, D]), sb("bo_bc", [128, D]), sb("br_bc", [128, E])
        bn_stats = sb("bn_stats", [128, 2 * B, 6])
        bn_mv = sb("bn_mv", [128, 2])
        bn_var, bn_rstd, bn_scale, bn_shift, bn_ms = (
            sb(n, [128, 1]) for n in ("bn_var", "bn_rstd", "bn_scale", "bn_shift", "bn_ms"))
        minus_half = sb("minus_half", [128, NT])
        ident, identb = sb("ident", [128, 128]), sb("identb", [128, 128], bf16)
        zero_b = sb("zero_b", [128, NT * E], bf16)
        ones_b, before = sb("ones_b", [128, 128], bf16), sb("before", [128, 128], bf16)
        rank_e = sb("rank_e", [128, NT, E])
        valid = sb("valid", [128, NT, E])
        far = sb("far", [128, NT])
        w1_sb = seq[:, 0:E * HID].rearrange("p (e n) -> p e n", e=E)
        w2_sb = seq[:, E * HID:2 * E * HID].rearrange("p (e n) -> p e n", e=E)
        W_LAST = -(-2 * E * HID // LP)
        b12, b12_rest, b12_rest2 = (t[0:E, 0:HID + D] for t in (xn_t, merged_t, q_rest))
        b12_part = sb("b12_part", [E, 3, HID + D], bf16)
        b12_rows = sb("b12_rows", [128, E, HID + D], bf16)
        pad_row = sb("pad_row", [128, ROW])
        pad_pos, pad_pos_i = sb("pad_pos", [128, E + 1]), sb("pad_pos_i", [128, E + 1], i32)
        region = sb("region", [128, E])
        lane = sb("lane", [128, 1])
        count1, tiles_f, tiles_i = sb("count1", [1, E]), sb("tiles_f", [1, E]), sb("tiles_i", [1, E], i32)
        tiles, cum, skip_e, zero_e = (sb(n, [1, E]) for n in ("tiles", "cum", "skip_e", "zero_e"))
        slot_f = k_part[0:1, :, :].rearrange("p a t -> p (a t)").bitcast(fp32)[:, 0:SLOTS * E]\
            .rearrange("p (s e) -> p s e", e=E)
        beyond = q_part[0:1, :, :].rearrange("p a t -> p (a t)").bitcast(fp32)[:, 0:SLOTS * E]\
            .rearrange("p (s e) -> p s e", e=E)
        beyond_w = o_un[0:1, :, :].rearrange("p a t -> p (a t)")[:, 0:SLOTS * E].rearrange("p (s e) -> p s e", e=E)
        slot_e, slot_r = sb("slot_e", [1, SLOTS]), sb("slot_r", [1, SLOTS])
        slot_e_i, slot_r_i = sb("slot_e_i", [1, SLOTS], i32), sb("slot_r_i", [1, SLOTS], i32)
        def of_ring(first, n):
            return p_ring[:, first:first + n]

        slot_rows = [of_ring(ROW * n, ROW) for n in range(4)]
        slot_xt = [of_ring(4 * ROW + D * n, D) for n in range(2)]
        slot_h = [of_ring(4 * ROW + 2 * D + HID * n, HID) for n in range(2)]
        slot_ht = [of_ring(4 * ROW + 2 * D + HID * (2 + n), HID) for n in range(2)]
        slot_y = [of_ring(4 * ROW + 2 * D + 4 * HID + D * n, D) for n in range(4)]

        psum = ctx.enter_context(nc.psum_tensor("psum", [128, 8, 512], fp32))
        st_bank = [psum[:, n, :] for n in range(N_ST)]
        mx_bank = [psum[:, N_ST + n, :] for n in range(N_MX)]
        o_bank = psum[:, 5, :]
        misc = psum[:, 6:8, :].rearrange("p a c -> p (a c)")
        misc_halves = psum[:, 6:8, 0:HALF]
        misc_b = misc.bitcast(bf16)

        s_tokw = sem("s_tokw")
        s_const = sem("s_const")
        s_w = sem("s_w")
        s_b12 = sem("s_b12")
        s_patch = [sem(f"s_patch{n}") for n in range(N_P)]
        s_tok = sem("s_tok")
        s_tok_y = sem("s_tok_y")
        s_tok_st = sem("s_tok_st")
        s_bn_pow = sem("s_bn_pow")
        s_pool_c = sem("s_pool_c")
        s_vec_c = sem("s_vec_c")
        s_st = sem("s_st")
        s_exp = sem("s_exp")
        s_pv = sem("s_pv")
        s_o = sem("s_o")
        s_mx = sem("s_mx")
        s_red = sem("s_red")
        s_max = sem("s_max")
        s_misc = sem("s_misc")
        s_free = sem("s_free")
        s_ht = sem("s_ht")
        s_ln = sem("s_ln")
        s_ln_p = sem("s_ln_p")
        s_ln2 = sem("s_ln2")
        s_ln2_p = sem("s_ln2_p")
        s_split = sem("s_split")
        s_qk_w = sem("s_qk_w")
        s_ld = [sem(f"s_ld{g}") for g in range(2)]
        s_mrow = sem("s_mrow")
        s_den = sem("s_den")
        s_rt = sem("s_rt")
        s_gate = sem("s_gate")
        s_rk = sem("s_rk")
        s_scat = sem("s_scat")
        s_tab = sem("s_tab")
        s_pad = sem("s_pad")
        s_in = [sem(f"s_in{n}") for n in range(4)]
        s_out = [sem(f"s_out{n}") for n in range(4)]
        s_fx = sem("s_fx")
        s_fxt = sem("s_fxt")
        s_f1 = sem("s_f1")
        s_fr = sem("s_fr")
        s_fh = sem("s_fh")
        s_fht = sem("s_fht")
        s_f2 = sem("s_f2")
        s_fy = sem("s_fy")

        s_apart_v = sem("s_apart_v")
        s_apart_p = sem("s_apart_p")

        FIRST_LOOP, LOOP_PAIRS = 1, (B - 3) // 2
        TASKS = (("V", 2), ("MAX1", 5), ("OT0", 9), ("HTOK", 14), ("OT1", 20), ("MT", 26), ("XNT", 32),
                 ("PROJ", 38), ("Q", 44), ("MAX0", 54), ("XN2T", 62), ("K", 68), ("LOGIT", 74), ("RANK", 84))
        STAGE = {"V": 1, "MAX1": 0, "OT0": -1, "HTOK": 2, "OT1": -1, "MT": -1, "XNT": 2,
                 "PROJ": -1, "Q": 2, "MAX0": 1, "XN2T": -1, "K": 2, "LOGIT": -1, "RANK": -1}

        def live(i, ahead):
            return not isinstance(i, int) or 0 <= i + ahead < B

        def tasks_before(i):
            def count(n):
                return sum(0 <= n + STAGE[name] < B for name, _ in TASKS)
            if isinstance(i, int):
                return sum(count(n) for n in range(-2, i))
            return (i - FIRST_LOOP) * len(TASKS) + sum(count(n) for n in range(-2, FIRST_LOOP))

        def number(i, task):
            k = 1
            for name, _ in TASKS:
                if name == task:
                    return tasks_before(i) + k
                k += live(i, STAGE[name])

        def run_bodies(engine, body):
            for i in range(-2, FIRST_LOOP):
                body(i, i % 2)
            with engine.Fori(0, LOOP_PAIRS) as v:
                for u in range(2):
                    body(v * 2 + (FIRST_LOOP + u), (FIRST_LOOP + u) % 2)
            for i in range(FIRST_LOOP + 2 * LOOP_PAIRS, B + 1):
                body(i, i % 2)

        def wait(engine, semaphore, value):
            if not isinstance(value, int) or value > 0:
                engine.wait_ge(semaphore, value)

        def wait_apart(engine, semaphore, value, counts):
            engine.wait_ge(semaphore, value)
            engine.sem_inc(counts, 1)

        def kn(kt):
            return LAST if kt == NT - 1 else D

        def step_of(s):
            p, kt, j = s // PASS, s % PASS // GH, s % GH
            return p // 2, p % 2, kt, GH * (p // 2) + j, j

        nc.disable_value_cache = True
        block = ctx.enter_context(nc.Block())

        @block.sync
        def _(sp):
            consts = ((tok_w_sb[:, :], tok_w), (tok_b_sb[:, :], tok_b.unsqueeze(1)))
            for dst, src in consts:
                sp.dma_start(dst, src).then_inc(s_tokw, 16)
            for c in range(NCH):
                if c >= N_P:
                    sp.wait_ge(s_tok, 2 * CH * (c - N_P + 1))
                for k in range(CONTEXT):
                    sp.dma_start(patches[FEAT * k:FEAT * (k + 1), c % N_P, :, :],
                                 x_t[:, CH * c:CH * (c + 1), k:k + L]).then_inc(s_patch[c % N_P], 16)
                if c == 0:
                    for dst, src in ((gamma_sb, gamma), (beta_sb, beta), (bq_sb, bq), (bk_sb, bk)):
                        sp.dma_start(dst[:, :], src.unsqueeze(1)).then_inc(s_const, 16)
                    for dst, src in ((bv_bc, bv), (bo_bc, bo), (br_bc, br)):
                        sp.dma_start(dst[:, :], src.partition_broadcast(128)).then_inc(s_const, 16)
                    for dst, src in ((wq_sb, wq), (wk_sb, wk), (wv_sb, wv), (wo_sb, wo), (wr_sb, wr)):
                        sp.dma_start(dst[:, :], src).then_inc(s_const, 16)
                    sp.dma_start(b12[:, 0:HID], b1).then_inc(s_const, 16)
                    sp.dma_start(b12[:, HID:HID + D], b2).then_inc(s_const, 16)
            sp.wait_ge(s_vec_c, 5)
            for n in range(3):
                sp.dma_start(b12_rows[n:n + 1, :, :], b12_part[:, n, :]).then_inc(s_b12, 16)

            def load_group(par, g):
                for dst, src, parts in ((q_rows, q_dram, Q_PARTS), (k_rows, k_dram, K_PARTS)):
                    for n, part in enumerate(parts):
                        sp.dma_start(dst[par][DH * n:DH * (n + 1), GH * g:GH * (g + 1), 0:L],
                                     src[64 * g:64 * (g + 1), part, :].rearrange("(h j) t -> j h t", j=DH))\
                          .then_inc(s_ld[g], 16)

            def body(i, par):
                if live(i, 1):
                    wait(sp, s_st, STEPS * i if live(i, -1) else 0)
                    load_group(1 - par, 1)
                if live(i, 0):
                    sp.wait_ge(s_free, number(i, "MAX1"))
                    for n in range(2):
                        sp.dma_start(q_rows[par][KR + n:KR + n + 1, GH:H, 0:L],
                                     max_rows[1][GH * n:GH * (n + 1), :]).then_inc(s_mrow, 16)
                if live(i, 1):
                    sp.wait_ge(s_free, number(i, "MAX0"))
                    for n in range(2):
                        sp.dma_start(q_rows[1 - par][KR + n:KR + n + 1, 0:GH, 0:L],
                                     max_rows[0][GH * n:GH * (n + 1), :]).then_inc(s_mrow, 16)
                if isinstance(i, int) and i == W_LAST + 2:
                    sp.wait_ge(s_ln2, W_LAST * 3 + 1)
                    sp.dma_start(w1_sb[:, :, :], w1.rearrange("e p n -> p e n")).then_inc(s_w, 16)
                    for e in range(E):
                        sp.dma_start(w2_sb[:, e, :].rearrange("p (j n) -> p j n", j=JH),
                                     w2[e].rearrange("(j p) n -> p j n", p=128)).then_inc(s_w, 16)
                if live(i, 2):
                    wait(sp, s_ld[1], (i + 2) * 192)
                    sp.wait_ge(s_split, (i + 2) * 6 + 3)
                    sp.dma_start(q_dram, q_part[:, :, :]).then_inc(s_qk_w, 16)
                    sp.wait_ge(s_split, (i + 2) * 6 + 6)
                    sp.dma_start(k_dram, k_part[:, :, :]).then_inc(s_qk_w, 16)
                    if live(i, 0):
                        sp.wait_ge(s_st, i * STEPS + STEPS // 2)
                    sp.wait_ge(s_qk_w, (i + 2) * 32 + 32)
                    load_group(par, 0)

            run_bodies(sp, body)

            sp.wait_ge(s_scat, B * NT * 16)
            sp.wait_ge(s_pad, (E + 1) * 16)
            sp.wait_ge(s_tab, 12)

            def load_slot(s, n):
                first = sp.value_load(slot_r_i[0:1, bass.ds(s, 1)], min_val=0, max_val=DEAD)
                sp.dma_start(slot_rows[n][:, :], rows_dram[bass.ds(first, D), :]).then_inc(s_in[n], 16)

            for s in range(4):
                load_slot(s, s)
            with sp.Fori(0, (SLOTS - 6) // 4) as v:
                for u in range(4):
                    sp.wait_ge(s_out[u], v * 16 + 16)
                    load_slot(v * 4 + (4 + u), u)
            done = (SLOTS - 6) // 4
            for s in range(4 + 4 * done, SLOTS):
                sp.wait_ge(s_out[s % 4], 16 * (s // 4))
                load_slot(s, s % 4)
            for n in range(4):
                sp.wait_ge(s_out[n], 16 * len(range(n, SLOTS, 4)))

        @block.gpsimd
        def _(pool):
            nc.gpsimd.memset(ident[:, :], 0.0)
            nc.gpsimd.memset(identb[:, :], 0.0)
            nc.gpsimd.memset(before[:, :], 1.0)
            nc.gpsimd.memset(valid[:, :, :], 1.0)
            nc.gpsimd.memset(far[:, :], 0.0)
            nc.gpsimd.memset(pad_row[:, :], 0.0).then_inc(s_pool_c, 1)
            pool.wait_ge(s_pool_c, 1)
            for m in (ident, identb):
                nc.gpsimd.affine_select(out=m[:, :], in_=m[:, :], compare_op=ALU.not_equal, fill=1.0, base=0,
                                        pattern=[[-1, 128]], channel_multiplier=1)
            nc.gpsimd.affine_select(out=before[:, :], in_=before[:, :], compare_op=ALU.is_gt, fill=0.0, base=0,
                                    pattern=[[1, 128]], channel_multiplier=-1)
            nc.gpsimd.affine_select(out=valid[:, :, :], in_=valid[:, :, :], compare_op=ALU.is_gt, fill=0.0,
                                    base=L, pattern=[[-D, NT], [0, E]], channel_multiplier=-1)
            nc.gpsimd.affine_select(out=far[:, :], in_=far[:, :], compare_op=ALU.is_gt, fill=float(FAR),
                                    base=L, pattern=[[-D, NT]], channel_multiplier=-1)
            nc.gpsimd.iota(tok_id[:, :], [[D, NT]], base=0, channel_multiplier=1,
                           allow_small_or_imprecise_dtypes=True)
            nc.gpsimd.iota(rank_e[:, :, :], [[0, NT], [-1, E]], base=E, channel_multiplier=0,
                           allow_small_or_imprecise_dtypes=True)
            nc.gpsimd.iota(region[:, :], [[CAP, E]], base=0, channel_multiplier=0,
                           allow_small_or_imprecise_dtypes=True)
            nc.gpsimd.iota(next_row[:, :], [[CAP, E]], base=0, channel_multiplier=0,
                           allow_small_or_imprecise_dtypes=True)
            nc.gpsimd.iota(lane[:, :], [[0, 1]], base=0, channel_multiplier=1,
                           allow_small_or_imprecise_dtypes=True)
            nc.gpsimd.iota(pad_row[:, ID:ID + 1].bitcast(i32), [[0, 1]], base=FAR, channel_multiplier=0)\
              .then_inc(s_pool_c, 1)
            pool.wait_ge(s_vec_c, 5)
            pool.wait_ge(s_tok_st, 2 * B + 2)
            nc.gpsimd.tensor_tensor(bn_rstd[:, :], bn_var[:, :], minus_half[:, 0:1], ALU.pow).then_inc(s_bn_pow, 1)

            def split(b, full, rest, part, k):
                nc.gpsimd.tensor_tensor(rest[:, :], full[:, :], part[:, 0, :], ALU.subtract).then_inc(s_split, 1)
                wait_apart(pool, s_split, b * 6 + (k + 1), s_apart_p)
                nc.gpsimd.tensor_scalar(part[:, 1, :], rest[:, :], 1.0, None, ALU.mult).then_inc(s_split, 1)
                pool.wait_ge(s_split, b * 6 + (k + 2))
                nc.gpsimd.tensor_tensor(part[:, 2, :], rest[:, :], part[:, 1, :], ALU.subtract).then_inc(s_split, 1)

            def body(i, par):
                if live(i, 2):
                    b = i + 2
                    pool.wait_ge(s_ln, b * 3 + 3)
                    nc.gpsimd.tensor_tensor(rstd[:, :], var_eps[:, :], minus_half[:, :], ALU.pow).then_inc(s_ln_p, 1)
                    wait_apart(pool, s_ln_p, b * 3 + 1, s_apart_p)
                    for t in range(NT):
                        last = nc.gpsimd.tensor_scalar(xn[:, t, :], h_cur[:, t, :], mv[:, t, 0:1], rstd[:, t:t + 1],
                                                       ALU.subtract, ALU.mult)
                    last.then_inc(s_ln_p, 1)
                    nc.gpsimd.tensor_tensor(seq[:, bass.ds(b * LP, LP)].rearrange("p (t d) -> p t d", t=NT),
                                            h_cur[:, :, :], bo_bc[:, :].unsqueeze(1).to_broadcast([128, NT, D]),
                                            ALU.add).then_inc(s_ln_p, 1)
                if live(i, -1):
                    r = i - 1
                    pool.wait_ge(s_ln2, r * 3 + 3)
                    nc.gpsimd.tensor_tensor(rstd2[:, :], var_eps2[:, :], minus_half[:, :], ALU.pow)\
                      .then_inc(s_ln2_p, 1)
                    wait_apart(pool, s_ln2_p, r * 2 + 1, s_apart_p)
                    for t in range(NT):
                        last = nc.gpsimd.tensor_scalar(rows[:, t, D:2 * D], rows[:, t, 0:D], mv2[:, t, 0:1],
                                                       rstd2[:, t:t + 1], ALU.subtract, ALU.mult)
                    last.then_inc(s_ln2_p, 1)
                if live(i, 2):
                    pool.wait_ge(s_free, number(i, "Q"))
                    split(b, q_full, q_rest, q_part, 0)
                    pool.wait_ge(s_free, number(i, "K"))
                    split(b, k_full, k_rest, k_part, 3)
                if live(i, -1):
                    pool.wait_ge(s_rk, r * 5 + 5)
                    wait_apart(pool, s_rt, r * 10 + 10, s_apart_p)
                    for t in range(NT):
                        pool.indirect_dma_start(
                            out=rows_dram, out_offset=bass.IndirectOffsetOnAxis(ap=pos_i[:, t:t + 1], axis=0),
                            in_=rows[:, t, :], in_offset=None, bounds_check=DEAD - 1, oob_is_err=False)\
                            .then_inc(s_scat, 16)

            run_bodies(pool, body)

            nc.gpsimd.iota(slot_f[:, :, :], [[1, SLOTS], [0, E]], base=0, channel_multiplier=0,
                           allow_small_or_imprecise_dtypes=True).then_inc(s_pool_c, 1)
            pool.wait_ge(s_tab, 2)
            for e in range(E + 1):
                pool.indirect_dma_start(
                    out=rows_dram, out_offset=bass.IndirectOffsetOnAxis(ap=pad_pos_i[:, e:e + 1], axis=0),
                    in_=pad_row[:, :], in_offset=None, bounds_check=DEAD + D - 1, oob_is_err=False)\
                    .then_inc(s_pad, 16)

            def store_slot(s, n, s4):
                pool.wait_ge(s_fy, s + 1)
                wait_apart(pool, s_in[n], s4 * 16 + 16, s_apart_p)
                pool.indirect_dma_start(
                    out=out_rows,
                    out_offset=bass.IndirectOffsetOnAxis(ap=slot_rows[n][:, ID:ID + 1].bitcast(i32), axis=0),
                    in_=slot_y[n][:, :], in_offset=None, bounds_check=NTOK - 1, oob_is_err=False)\
                    .then_inc(s_out[n], 16)

            with pool.Fori(0, SLOTS // 4) as v:
                for u in range(4):
                    store_slot(v * 4 + u, u, v)
            for s in range(SLOTS // 4 * 4, SLOTS):
                store_slot(s, s % 4, s // 4)

        @block.scalar
        def _(act):
            act.wait_ge(s_tokw, 16 * 2)
            for n in range(2 * B):
                act.wait_ge(s_tok, n + 1)
                b, half = n // 2, n % 2
                nc.scalar.activation(seq[:, b * LP + half * HALF:b * LP + (half + 1) * HALF],
                                     psum[:, n % 8, 0:HALF], ACT.Relu, bias=tok_b_sb[:, 0:1]).then_inc(s_tok_y, 1)
            act.wait_ge(s_tok_st, 2 * B + 5)
            act.wait_ge(s_vec_c, 5)

            def body(i, par):
                for s in range(STEPS + 1):
                    if s < STEPS and live(i, 0):
                        g, qh, kt, h, j = step_of(s)
                        G = s // GH
                        if j == 0:
                            wait(act, s_pv, i * GROUPS + (G - N_P + 1))
                        act.wait_ge(s_st, i * STEPS + (s + 1))
                        nc.scalar.activation(probs[0:kn(kt), G % N_P, j, :], st_bank[s % N_ST][0:kn(kt), 0:HALF],
                                             ACT.Exp).then_inc(s_exp, 1)
                    if s % PASS == 4:
                        b, p = (i, s // PASS - 1) if s >= PASS else (i - 1, 3)
                        if live(i, b if s < 0 else (0 if s >= PASS else -1)):
                            act.wait_ge(s_pv, b * GROUPS + NT * (p + 1))
                            if p == 0 and live(i, -1):
                                act.wait_ge(s_misc, number(i, "OT1"))
                            nc.scalar.copy(o_un[:, p // 2, p % 2 * HALF:(p % 2 + 1) * HALF], o_bank[:, 0:HALF])\
                              .then_inc(s_o, 1)
                    if s == 0 and live(i, 2):
                        wait(act, s_misc, number(i - 1, "HTOK") if live(i, 1) else 0)
                        nc.scalar.activation(h_t[:, 0:L], seq[:, bass.ds((i + 2) * LP, L)], ACT.Identity,
                                             bias=bn_shift[:, 0:1], scale=bn_scale[:, 0:1]).then_inc(s_ht, 1)
                    if s == 7 and live(i, 0):
                        max_evac(i, i, 1, "MAX1")
                    if s == 16 and live(i, 2):
                        act.wait_ge(s_misc, number(i, "HTOK"))
                        wait(act, s_ln_p, (i + 2) * 3)
                        nc.scalar.copy(h_cur[:, :, :].rearrange("p t d -> p (t d)"), misc[:, 0:LP])\
                          .then_inc(s_free, 1)
                    if s == 28 and live(i, -1):
                        act.wait_ge(s_misc, number(i, "MT"))
                        nc.scalar.copy(merged_t[:, :], misc[:, 0:LP]).then_inc(s_free, 1)
                    if s == 34 and live(i, 2):
                        act.wait_ge(s_misc, number(i, "XNT"))
                        nc.scalar.copy(xn_t[:, :], misc[:, 0:LP]).then_inc(s_free, 1)
                    if s in (47, 71) and live(i, 2):
                        name, full, part, bias, scale = (("Q", q_full, q_part, bq4, SCALE) if s == 47 else
                                                         ("K", k_full, k_part, bk_sb, 1.0))
                        act.wait_ge(s_misc, number(i, name))
                        wait(act, s_qk_w, (i + 2) * 32)
                        nc.scalar.activation(full[:, :].rearrange("p (a t) -> p a t", a=2), misc_halves,
                                             ACT.Identity, bias=bias[:, 0:1], scale=scale)
                        nc.scalar.activation(part[:, 0, :].rearrange("p (a t) -> p a t", a=2), misc_halves,
                                             ACT.Identity, bias=bias[:, 0:1], scale=scale).then_inc(s_free, 1)
                    if s == 56 and live(i, 1):
                        max_evac(i, i + 1, 0, "MAX0")
                    if s == 64 and live(i, -1):
                        act.wait_ge(s_misc, number(i, "XN2T"))
                        nc.scalar.copy(xn2_t[:, :], misc[:, 0:LP]).then_inc(s_free, 1)
                    if s == 80 and live(i, -1):
                        act.wait_ge(s_rt, (i - 1) * 10 + 7)
                        nc.scalar.activation(g_exp[:, :], g_diff[:, :], ACT.Exp).then_inc(s_gate, 1)

            def max_evac(i, b, g, name):
                act.wait_ge(s_misc, number(i, name))
                wait(act, s_mrow, (b - 1) * 64 + 32 * (g + 1) if not isinstance(b, int) or b > 0 else 0)
                nc.scalar.copy(max_rows[g][:, :], misc_b[0:2 * GH, 0:L]).then_inc(s_free, 1)

            run_bodies(act, body)

            def relu(s, n):
                act.wait_ge(s_f1, s + 1)
                if not isinstance(s, int) or s >= 2:
                    act.wait_ge(s_fh, s - 1)
                nc.scalar.activation(slot_h[n % 2][:, :], psum[:, 2 + n % 2, :], ACT.Relu).then_inc(s_fr, 1)

            def xt_evac(s, n):
                act.wait_ge(s_fx, s + 1)
                if not isinstance(s, int) or s >= 2:
                    act.wait_ge(s_f1, s - 1)
                nc.scalar.copy(slot_xt[n % 2][:, :], psum[:, n % 2, 0:D]).then_inc(s_fxt, 1)

            xt_evac(0, 0)
            relu(0, 0)
            xt_evac(1, 1)
            for s in range(1, 5):
                relu(s, s)
                xt_evac(s + 1, s + 1)
            with act.Fori(1, (SLOTS - 2) // 4) as v:
                for u in range(4):
                    relu(v * 4 + (1 + u), 1 + u)
                    xt_evac(v * 4 + (2 + u), 2 + u)
            relu(SLOTS - 1, SLOTS - 1)

        @block.vector
        def _(dve):
            nc.vector.memset(minus_half[:, :], -0.5)
            nc.vector.memset(ones_b[:, :], 1.0)
            nc.vector.memset(zero_b[:, :], 0.0)
            nc.vector.memset(h_t[:, L:LP], 0.0)
            nc.vector.memset(o_un[:, :, L:LP], 1.0)
            nc.vector.memset(rows[:, :, 2 * D:ROW], 0.0)
            nc.vector.memset(zero_e[:, :], 0.0)
            nc.vector.memset(b12_rows[:, :, :], 0.0)
            for n in range(2):
                nc.vector.memset(q_rows[n][0:KR, :, L:LP], 0.0)
                nc.vector.memset(k_rows[n][KR:KM, :, :], 1.0)
                nc.vector.memset(values[n][:, :, :, DH:32], 1.0)
            dve.wait_ge(s_const, 16 * 14)
            nc.vector.tensor_scalar(bq4[:, :], bq_sb[:, :], SCALE, None, ALU.mult)
            nc.vector.tensor_copy(b12_part[:, 0, :], b12[:, :]).then_inc(s_vec_c, 1)
            dve.wait_ge(s_vec_c, 1)
            nc.vector.tensor_tensor(b12_rest[:, :], b12[:, :], b12_part[:, 0, :], ALU.subtract).then_inc(s_vec_c, 1)
            dve.wait_ge(s_vec_c, 2)
            nc.vector.tensor_copy(b12_part[:, 1, :], b12_rest[:, :]).then_inc(s_vec_c, 1)
            dve.wait_ge(s_vec_c, 3)
            nc.vector.tensor_tensor(b12_rest2[:, :], b12_rest[:, :], b12_part[:, 1, :], ALU.subtract)\
              .then_inc(s_vec_c, 1)
            dve.wait_ge(s_vec_c, 4)
            nc.vector.tensor_copy(b12_part[:, 2, :], b12_rest2[:, :]).then_inc(s_vec_c, 1)

            for n in range(2 * B):
                dve.wait_ge(s_tok_y, n + 1)
                b, half = n // 2, n % 2
                nc.vector.bn_stats(bn_stats[:, n, :],
                                   seq[:, b * LP + half * HALF:b * LP + (half + 1) * HALF]).then_inc(s_tok_st, 1)
            dve.wait_ge(s_tok_st, 2 * B)
            nc.vector.bn_aggr(bn_mv[:, :], bn_stats[:, :, :]).then_inc(s_tok_st, 1)
            dve.wait_ge(s_tok_st, 2 * B + 1)
            nc.vector.tensor_scalar(bn_var[:, :], bn_mv[:, 1:2], EPS, None, ALU.add).then_inc(s_tok_st, 1)
            dve.wait_ge(s_bn_pow, 1)
            nc.vector.tensor_tensor(bn_scale[:, :], bn_rstd[:, :], gamma_sb[:, :], ALU.mult).then_inc(s_tok_st, 1)
            dve.wait_ge(s_tok_st, 2 * B + 3)
            nc.vector.tensor_tensor(bn_ms[:, :], bn_mv[:, 0:1], bn_scale[:, :], ALU.mult).then_inc(s_tok_st, 1)
            dve.wait_ge(s_tok_st, 2 * B + 4)
            nc.vector.tensor_tensor(bn_shift[:, :], beta_sb[:, :], bn_ms[:, :], ALU.subtract).then_inc(s_tok_st, 1)
            dve.wait_ge(s_pool_c, 2)

            def layer_stats(b, tiles_of, st, mean_var, out_var, counter, after):
                for t in range(NT):
                    last = nc.vector.bn_stats(st[:, t, :], tiles_of[:, t, 0:D])
                last.then_inc(counter, 1)
                wait_apart(dve, counter, b * 3 + 1, s_apart_v)
                for t in range(NT):
                    last = nc.vector.bn_aggr(mean_var[:, t, :], st[:, t, :])
                last.then_inc(counter, 1)
                dve.wait_ge(counter, b * 3 + 2)
                nc.vector.tensor_scalar(out_var[:, :], mean_var[:, :, 1], EPS, None, ALU.add).then_inc(counter, 1)

            def maxima(b, g):
                k = 3 * g
                dve.wait_ge(s_red, b * STEPS + STEPS // 2 * (g + 1))
                nc.vector.tensor_reduce(neg_max[:, 24 * g:24 * (g + 1)],
                                        half_max[:, 48 * g:48 * (g + 1)].rearrange("p (n a) -> p n a", a=2),
                                        AX.X, ALU.max, negate=True).then_inc(s_max, 1)
                dve.wait_ge(s_max, b * 6 + (k + 1))
                full = neg_max[:, 24 * g:24 * (g + 1)].rearrange("p (h t) -> p t h", h=GH)
                nc.vector.tensor_copy(max_parts[:, g, :, 0, :], full).then_inc(s_max, 1)
                dve.wait_ge(s_max, b * 6 + (k + 2))
                nc.vector.tensor_tensor(max_parts[:, g, :, 1, :], full, max_parts[:, g, :, 0, :], ALU.subtract)\
                  .then_inc(s_max, 1)

            def normalise(i, r, c):
                dve.wait_ge(s_misc, number(i, f"OT{c}"))
                o = misc[:, 0:LP].rearrange("p (n c) -> p n c", c=32)
                nc.vector.reciprocal(r_den[:, :], o[:, :, DH]).then_inc(s_den, 1)
                dve.wait_ge(s_den, r * 2 + (c + 1))
                nc.vector.tensor_tensor(
                    merged[:, 3 * c:3 * (c + 1), :].rearrange("p t (h d) -> p (t h) d", h=H), o[:, :, 0:DH],
                    r_den[:, :].unsqueeze(2).to_broadcast([128, NT // 2 * H, DH]), ALU.mult).then_inc(s_free, 1)

            def router(i, r):
                per = lambda a: a[:, :].unsqueeze(2).to_broadcast([128, NT, E])
                dve.wait_ge(s_misc, number(i, "LOGIT"))
                nc.vector.tensor_tensor(logits[:, :, :], misc[:, 0:NT * E].rearrange("p (t e) -> p t e", t=NT),
                                        br_bc[:, :].unsqueeze(1).to_broadcast([128, NT, E]), ALU.add)\
                  .then_inc(s_free, 1)
                dve.wait_ge(s_free, number(i, "LOGIT"))
                nc.vector.reduce_max(top[:, :], logits[:, :, :], AX.X).then_inc(s_rt, 1)
                dve.wait_ge(s_rt, r * 10 + 1)
                nc.vector.tensor_tensor(scored[:, :, :], logits[:, :, :], per(top), ALU.is_equal).then_inc(s_rt, 1)
                dve.wait_ge(s_rt, r * 10 + 2)
                nc.vector.tensor_tensor(scored2[:, :, :], scored[:, :, :], rank_e[:, :, :], ALU.mult)\
                  .then_inc(s_rt, 1)
                dve.wait_ge(s_rt, r * 10 + 3)
                nc.vector.reduce_max(best[:, :], scored2[:, :, :], AX.X).then_inc(s_rt, 1)
                dve.wait_ge(s_rt, r * 10 + 4)
                nc.vector.tensor_tensor(picked[:, :, :], rank_e[:, :, :], per(best), ALU.is_equal).then_inc(s_rt, 1)
                dve.wait_ge(s_rt, r * 10 + 5)
                nc.vector.tensor_tensor(onehot[:, :, :], picked[:, :, :], valid[:, :, :], ALU.mult).then_inc(s_rt, 1)
                nc.vector.tensor_tensor(g_diff[:, :], top[:, :], top[:, :], ALU.subtract).then_inc(s_rt, 1)

            def gates(r):
                dve.wait_ge(s_gate, r + 1)
                nc.vector.reciprocal(g_inv[:, :], g_exp[:, :]).then_inc(s_rt, 1)
                dve.wait_ge(s_rt, r * 10 + 8)
                nc.vector.tensor_tensor(rows[:, :, GATE], g_exp[:, :], g_inv[:, :], ALU.mult).then_inc(s_rt, 1)

            def ranks(i, r):
                dve.wait_ge(s_misc, number(i, "RANK"))
                nc.vector.tensor_tensor(place[:, :, :], misc[:, 0:NT * E].rearrange("p (t e) -> p t e", t=NT),
                                        next_row[:, :].unsqueeze(1).to_broadcast([128, NT, E]), ALU.add)\
                  .then_inc(s_rk, 1)
                dve.wait_ge(s_rk, r * 5 + 1)
                nc.vector.tensor_tensor(next_row[:, :], misc[:, 512:512 + E], next_row[:, :], ALU.add)\
                  .then_inc(s_free, 1)
                nc.vector.tensor_tensor(place1[:, :, :], place[:, :, :], onehot[:, :, :], ALU.mult).then_inc(s_rk, 1)
                dve.wait_ge(s_rk, r * 5 + 2)
                nc.vector.reduce_sum(pos[:, :], place1[:, :, :], AX.X).then_inc(s_rk, 1)
                dve.wait_ge(s_rk, r * 5 + 3)
                nc.vector.tensor_tensor(pos_i[:, :], pos[:, :], far[:, :], ALU.add).then_inc(s_rk, 1)
                nc.vector.tensor_copy(rows[:, :, ID].bitcast(i32), tok_id[:, :]).then_inc(s_rk, 1)
                dve.wait_ge(s_rk, r * 5 + 5)
                nc.vector.tensor_scalar(tok_id[:, :], tok_id[:, :], float(L), None, ALU.add).then_inc(s_rt, 1)

            def body(i, par):
                for s in range(STEPS):
                    if live(i, 1):
                        dve.wait_ge(s_mx, (i + 1) * STEPS + (s + 1))
                        nc.vector.tensor_reduce(half_max[:, s:s + 1], mx_bank[s % N_MX][:, 0:HALF], AX.X, ALU.max)\
                          .then_inc(s_red, 1)
                        if s % 48 == 47:
                            maxima(i + 1, s // 48)
                    if s == 5 and live(i, 1):
                        dve.wait_ge(s_misc, number(i, "V"))
                        nc.vector.tensor_tensor(
                            values[1 - par][:, :, :, 0:DH], misc[:, 0:LP].rearrange("p (t h d) -> p t h d", t=NT, h=H),
                            bv_bc[:, :].rearrange("p (h d) -> p h d", h=H).unsqueeze(1).to_broadcast([128, NT, H, DH]),
                            ALU.add).then_inc(s_free, 1)
                    if s == 12 and live(i, -1):
                        normalise(i, i - 1, 0)
                    if s == 18 and live(i, 2):
                        dve.wait_ge(s_free, number(i, "HTOK"))
                        layer_stats(i + 2, h_cur, stats, mv, var_eps, s_ln, None)
                    if s == 23 and live(i, -1):
                        normalise(i, i - 1, 1)
                    if s == 41 and live(i, -1):
                        r = i - 1
                        dve.wait_ge(s_misc, number(i, "PROJ"))
                        dve.wait_ge(s_ln_p, r * 3 + 3)
                        wait(dve, s_scat, r * (NT * 16))
                        nc.vector.tensor_tensor(rows[:, :, 0:D], misc[:, 0:LP].rearrange("p (t d) -> p t d", t=NT),
                                                seq[:, bass.ds(r * LP, LP)].rearrange("p (t d) -> p t d", t=NT),
                                                ALU.add).then_inc(s_free, 1)
                        dve.wait_ge(s_free, number(i, "PROJ"))
                        layer_stats(r, rows, stats2, mv2, var_eps2, s_ln2, None)
                    if s == 77 and live(i, -1):
                        router(i, i - 1)
                    if s == 86 and live(i, -1):
                        gates(i - 1)
                    if s == 88 and live(i, -1):
                        ranks(i, i - 1)

            run_bodies(dve, body)

            dve.wait_ge(s_pool_c, 3)
            nc.vector.tensor_scalar(pad_pos[:, 0:E], next_row[:, :], lane[:, 0:1], None, ALU.add)
            nc.vector.tensor_scalar(pad_pos[:, E:E + 1], lane[:, :], float(DEAD), None, ALU.add).then_inc(s_tab, 1)
            dve.wait_ge(s_tab, 1)
            nc.vector.tensor_copy(pad_pos_i[:, :], pad_pos[:, :]).then_inc(s_tab, 1)
            nc.vector.tensor_tensor(count1[:, :], next_row[0:1, :], region[0:1, :], ALU.subtract).then_inc(s_tab, 1)
            dve.wait_ge(s_tab, 3)
            nc.vector.tensor_scalar(tiles_f[:, :], count1[:, :], 1.0 / D, (D - 1) / D - (D - 1) / (2 * D),
                                    ALU.mult, ALU.add).then_inc(s_tab, 1)
            dve.wait_ge(s_tab, 4)
            nc.vector.tensor_copy(tiles_i[:, :], tiles_f[:, :]).then_inc(s_tab, 1)
            dve.wait_ge(s_tab, 5)
            nc.vector.tensor_copy(tiles[:, :], tiles_i[:, :]).then_inc(s_tab, 1)
            dve.wait_ge(s_tab, 6)
            nc.vector.tensor_tensor_scan(cum[:, :], tiles[:, :], zero_e[:, :], 0.0, ALU.add, ALU.add)
            nc.vector.tensor_scalar(skip_e[:, :], tiles[:, :], -float(D), float(CAP), ALU.mult, ALU.add)\
              .then_inc(s_tab, 1)
            dve.wait_ge(s_tab, 7)
            bc = lambda a: a[:, :].unsqueeze(1).to_broadcast([1, SLOTS, E])
            nc.vector.tensor_tensor(beyond[:, :, :], slot_f[:, :, :], bc(cum), ALU.is_ge).then_inc(s_tab, 1)
            dve.wait_ge(s_tab, 8)
            nc.vector.tensor_tensor(beyond_w[:, :, :], beyond[:, :, :], bc(skip_e), ALU.mult)
            nc.vector.reduce_sum(slot_e[:, :], beyond[:, :, :], AX.X).then_inc(s_tab, 1)
            dve.wait_ge(s_tab, 9)
            nc.vector.reduce_sum(slot_r[:, :], beyond_w[:, :, :], AX.X)
            nc.vector.tensor_scalar(slot_e_i[:, :], slot_e[:, :], float(E - 1), None, ALU.min).then_inc(s_tab, 1)
            dve.wait_ge(s_tab, 10)
            nc.vector.scalar_tensor_tensor(slot_r[:, :], slot_f[:, :, 0], float(D), slot_r[:, :], ALU.mult, ALU.add)\
              .then_inc(s_tab, 1)
            dve.wait_ge(s_tab, 11)
            nc.vector.tensor_scalar(slot_r_i[:, :], slot_r[:, :], float(DEAD), None, ALU.min).then_inc(s_tab, 1)

            def ht_evac(s, n):
                dve.wait_ge(s_fh, s + 1)
                if not isinstance(s, int) or s >= 2:
                    dve.wait_ge(s_f2, s - 1)
                nc.vector.tensor_copy(slot_ht[n % 2][:, :], psum[:, 4 + n % 2, :]).then_inc(s_fht, 1)

            def result(s, n, s4):
                dve.wait_ge(s_f2, s + 1)
                dve.wait_ge(s_in[n % 4], s4 * 16 + 16)
                if not isinstance(s4, int) or s4 > 0:
                    dve.wait_ge(s_out[n % 4], s4 * 16)
                nc.vector.scalar_tensor_tensor(slot_y[n % 4][:, :], psum[:, 6 + n % 2, 0:D],
                                               slot_rows[n % 4][:, GATE:GATE + 1], slot_rows[n % 4][:, 0:D],
                                               ALU.mult, ALU.add).then_inc(s_fy, 1)

            for s in range(4):
                ht_evac(s, s)
                result(s, s, 0)
            with dve.Fori(1, SLOTS // 4) as v:
                for u in range(4):
                    ht_evac(v * 4 + u, u)
                    result(v * 4 + u, u, v)
            for s in range(SLOTS // 4 * 4, SLOTS):
                ht_evac(s, s)
                result(s, s, s // 4)

        @block.tensor
        def _(pe):
            pe.wait_ge(s_tokw, 16 * 2)
            for n in range(2 * B):
                c, b, half = n // (2 * CH), n // 2, n % 2
                if n % (2 * CH) == 0:
                    pe.wait_ge(s_patch[c % N_P], 16 * CONTEXT * (c // N_P + 1))
                if n >= 8:
                    pe.wait_ge(s_tok_y, n - 7)
                nc.tensor.matmul(psum[:, n % 8, 0:HALF], tok_w_sb[:, :],
                                 patches[:, c % N_P, b % CH, half * HALF:(half + 1) * HALF],
                                 start=True, stop=True).then_inc(s_tok, 1)
            pe.wait_ge(s_tok_y, 2 * B)
            pe.wait_ge(s_pool_c, 2)
            pe.wait_ge(s_vec_c, 5)
            pe.wait_ge(s_const, 16 * 14)
            pe.wait_ge(s_b12, 16 * 3)

            def transposes(src):
                for t in range(NT):
                    last = nc.tensor.transpose(misc[:, D * t:D * (t + 1)], src(t), ident[:, :])
                return last

            def task(i, par, name):
                wait(pe, s_free, number(i, name) - 1)
                if name == "V":
                    for t in range(NT):
                        last = nc.tensor.matmul(misc[:, D * t:D * (t + 1)], xn_t[:, D * t:D * (t + 1)], wv_sb[:, :],
                                                start=True, stop=True)
                elif name in ("MAX0", "MAX1"):
                    g = int(name[3])
                    pe.wait_ge(s_max, (i + (1 - g)) * 6 + 3 * (g + 1))
                    for t in range(NT):
                        last = nc.tensor.transpose(misc_b[0:2 * GH, D * t:D * (t + 1)],
                                                   max_parts[:, g, t, :, :].rearrange("p a h -> p (a h)"), identb[:, :])
                elif name in ("OT0", "OT1"):
                    c = int(name[2])
                    pe.wait_ge(s_o, (i - 1) * 4 + 4)
                    for n in range(6):
                        t, g = 3 * c + n // 2, n % 2
                        last = nc.tensor.transpose(misc[:, D * n:D * (n + 1)], o_un[:, g, D * t:D * (t + 1)],
                                                   ident[:, :])
                elif name == "HTOK":
                    pe.wait_ge(s_ht, (i + 2) + 1)
                    last = transposes(lambda t: h_t[:, D * t:D * (t + 1)])
                elif name == "MT":
                    last = transposes(lambda t: merged[:, t, :])
                elif name == "XNT":
                    pe.wait_ge(s_ln_p, (i + 2) * 3 + 2)
                    last = transposes(lambda t: xn[:, t, :])
                elif name == "PROJ":
                    for t in range(NT):
                        last = nc.tensor.matmul(misc[:, D * t:D * (t + 1)], merged_t[:, D * t:D * (t + 1)],
                                                wo_sb[:, :], start=True, stop=True)
                elif name in ("Q", "K"):
                    for half in range(2):
                        last = nc.tensor.matmul(misc_halves[:, half, :], (wq_sb if name == "Q" else wk_sb)[:, :],
                                                xn_t[:, half * HALF:(half + 1) * HALF], start=True, stop=True)
                elif name == "XN2T":
                    pe.wait_ge(s_ln2_p, (i - 1) * 2 + 2)
                    last = transposes(lambda t: rows[:, t, D:2 * D])
                elif name == "LOGIT":
                    for t in range(NT):
                        last = nc.tensor.matmul(misc[:, E * t:E * (t + 1)], xn2_t[:, D * t:D * (t + 1)], wr_sb[:, :],
                                                start=True, stop=True)
                elif name == "RANK":
                    pe.wait_ge(s_rt, (i - 1) * 10 + 6)
                    nc.tensor.matmul(misc[:, 0:NT * E], before[:, :], onehot[:, :, :].rearrange("p t e -> p (t e)"),
                                     start=True, stop=False)
                    for t in range(NT - 1):
                        nc.tensor.matmul(misc[:, E * (t + 1):NT * E].rearrange("p (t e) -> p t e", e=E), ones_b[:, :],
                                         onehot[:, t:t + 1, :].to_broadcast([128, NT - 1 - t, E]),
                                         start=False, stop=False)
                    nc.tensor.matmul(misc[:, 0:NT * E], ones_b[:, :], zero_b[:, :], start=False, stop=True)
                    for t in range(NT):
                        last = nc.tensor.matmul(misc[:, 512:512 + E], ones_b[:, :], onehot[:, t, :],
                                                start=t == 0, stop=t == NT - 1)
                last.then_inc(s_misc, 1)

            def weigh(b, par, G):
                p, kt = G // NT, G % NT
                pe.wait_ge(s_exp, b * STEPS + GH * (G + 1))
                if kt == 0:
                    wait(pe, s_o, b * 4 + p)
                for j in range(GH):
                    last = nc.tensor.matmul(o_bank[32 * j:32 * (j + 1), 0:HALF],
                                            values[par][0:kn(kt), kt, GH * (p // 2) + j, :],
                                            probs[0:kn(kt), G % N_P, j, :], start=kt == 0, stop=kt == NT - 1)
                last.then_inc(s_pv, 1)

            def body(i, par):
                for s in range(STEPS):
                    if live(i, 0):
                        g, qh, kt, h, j = step_of(s)
                        if s % 48 == 0:
                            pe.wait_ge(s_mrow, i * 64 + 32 * (g + 1))
                        wait(pe, s_exp, i * STEPS + (s + 1 - N_ST))
                        nc.tensor.matmul(st_bank[s % N_ST][0:kn(kt), 0:HALF],
                                         k_rows[par][0:KM, h, D * kt:D * kt + kn(kt)],
                                         q_rows[par][0:KM, h, qh * HALF:(qh + 1) * HALF],
                                         start=True, stop=True).then_inc(s_st, 1)
                    if live(i, 1):
                        b, h, t, half = i + 1, s // 12, s % 12 // 2, s % 2
                        if s % 48 == 0:
                            pe.wait_ge(s_ld[s // 48], b * 192 + 192)
                        wait(pe, s_red, b * STEPS + (s + 1 - N_MX))
                        nc.tensor.matmul(mx_bank[s % N_MX][:, 0:HALF], q_rows[1 - par][0:KR, h, D * t:D * (t + 1)],
                                         k_rows[1 - par][0:KR, h, half * HALF:(half + 1) * HALF],
                                         start=True, stop=True).then_inc(s_mx, 1)
                    if s == 2 and live(i, -1):
                        weigh(i - 1, 1 - par, GROUPS - 1)
                    if s > 2 and s % GH == 2 and live(i, 0):
                        weigh(i, par, s // GH - 1)
                    for name, at in TASKS:
                        if at == s and live(i, STAGE[name]):
                            task(i, par, name)

            run_bodies(pe, body)

            pe.wait_ge(s_tab, 12)
            pe.wait_ge(s_w, 16 * (E + 1))

            def x_t_slot(s, n, s4):
                pe.wait_ge(s_in[n % 4], s4 * 16 + 16)
                if not isinstance(s, int) or s >= 2:
                    pe.wait_ge(s_fxt, s - 1)
                nc.tensor.transpose(psum[:, n % 2, 0:D], slot_rows[n % 4][:, D:2 * D], ident[:, :]).then_inc(s_fx, 1)

            def layer1(s, n):
                e = pe.value_load(slot_e_i[0:1, bass.ds(s, 1)], min_val=0, max_val=E - 1)
                pe.wait_ge(s_fxt, s + 1)
                if not isinstance(s, int) or s >= 2:
                    pe.wait_ge(s_fr, s - 1)
                nc.tensor.matmul(psum[:, 2 + n % 2, :], slot_xt[n % 2][:, :], w1_sb[:, bass.ds(e, 1), :],
                                 start=True, stop=False)
                nc.tensor.matmul(psum[:, 2 + n % 2, :], ones_b[:, :], b12_rows[:, bass.ds(e, 1), 0:HID],
                                 start=False, stop=True).then_inc(s_f1, 1)

            def h_t_slot(s, n):
                pe.wait_ge(s_fr, s + 1)
                if not isinstance(s, int) or s >= 2:
                    pe.wait_ge(s_fht, s - 1)
                for k in range(JH):
                    last = nc.tensor.transpose(psum[:, 4 + n % 2, D * k:D * (k + 1)],
                                               slot_h[n % 2][:, D * k:D * (k + 1)], ident[:, :])
                last.then_inc(s_fh, 1)

            def layer2(s, n):
                e = pe.value_load(slot_e_i[0:1, bass.ds(s, 1)], min_val=0, max_val=E - 1)
                pe.wait_ge(s_fht, s + 1)
                if not isinstance(s, int) or s >= 2:
                    pe.wait_ge(s_fy, s - 1)
                for k in range(JH):
                    nc.tensor.matmul(psum[:, 6 + n % 2, 0:D], slot_ht[n % 2][:, D * k:D * (k + 1)],
                                     w2_sb[:, bass.ds(e, 1), D * k:D * (k + 1)], start=k == 0, stop=False)
                nc.tensor.matmul(psum[:, 6 + n % 2, 0:D], ones_b[:, :], b12_rows[:, bass.ds(e, 1), HID:HID + D],
                                 start=False, stop=True).then_inc(s_f2, 1)

            x_t_slot(0, 0, 0)
            layer1(0, 0)
            x_t_slot(1, 1, 0)

            def turn(v, u):
                h_t_slot(v * 4 + u, u)
                layer1(v * 4 + (1 + u), 1 + u)
                layer2(v * 4 + u, u)
                x_t_slot(v * 4 + (2 + u), 2 + u, v + (2 + u) // 4)

            for u in range(4):
                turn(0, u)
            with pe.Fori(1, (SLOTS - 2) // 4) as v:
                for u in range(4):
                    turn(v, u)
            h_t_slot(SLOTS - 2, SLOTS - 2)
            layer1(SLOTS - 1, SLOTS - 1)
            layer2(SLOTS - 2, SLOTS - 2)
            h_t_slot(SLOTS - 1, SLOTS - 1)
            layer2(SLOTS - 1, SLOTS - 1)


def kernel(**inputs):
    import numpy as np
    import concourse.bacc as bacc
    from concourse.bass_utils import run_bass_kernel_spmd

    def a(name):
        return np.asarray(inputs[name])

    arrays = {
        "x_t": a("x").transpose(2, 0, 1),
        "tok_w": a("L0_tok_W").T, "tok_b": a("L0_tok_b"), "gamma": a("L0_tok_gamma"), "beta": a("L0_tok_beta"),
        "wq": a("L0_attn_Wq").T, "bq": a("L0_attn_bq"), "wk": a("L0_attn_Wk").T, "bk": a("L0_attn_bk"),
        "wv": a("L0_attn_Wv").T, "bv": a("L0_attn_bv"), "wo": a("L0_attn_Wo").T, "bo": a("L0_attn_bo"),
        "wr": a("L0_ffn_Wr"), "br": a("L0_ffn_br"), "w1": a("L0_ffn_W1"), "b1": a("L0_ffn_b1"),
        "w2": a("L0_ffn_W2"), "b2": a("L0_ffn_b2"),
    }
    arrays = {f"in_{n}_dram": np.ascontiguousarray(v) for n, v in arrays.items()}
    nc = bacc.Bacc("TRN2", target_bir_lowering=False, num_devices=1)
    args = [nc.dram_tensor(n, v.shape, mybir.dt.from_np(v.dtype), kind="ExternalInput").ap()
            for n, v in arrays.items()]
    b, frames, feat = inputs["x"].shape
    channels, taps = inputs["L0_tok_W"].shape
    shape = (b, frames - taps // feat + 1, channels)
    args.append(nc.dram_tensor("out_dram", shape, mybir.dt.float32, kind="ExternalOutput").ap())
    audio_tower(nc, *args)
    return run_bass_kernel_spmd(nc, [arrays], core_ids=[0]).results[0]["out_dram"]
```

```python
import concourse.bass as bass
from concourse import mybir
from contextlib import ExitStack


def audio_tower(
    nc: bass.Bass,
    x_t: bass.AP,
    tok_w: bass.AP,
    tok_b: bass.AP,
    gamma: bass.AP,
    beta: bass.AP,
    wq: bass.AP,
    bq: bass.AP,
    wk: bass.AP,
    bk: bass.AP,
    wv: bass.AP,
    bv: bass.AP,
    wo: bass.AP,
    bo: bass.AP,
    wr: bass.AP,
    br: bass.AP,
    w1: bass.AP,
    b1: bass.AP,
    w2: bass.AP,
    b2: bass.AP,
    out: bass.AP,
):
    fp32 = mybir.dt.float32
    bf16 = mybir.dt.bfloat16
    i32 = mybir.dt.int32
    ALU = mybir.AluOpType
    ACT = mybir.ActivationFunctionType
    AX = mybir.AxisListType

    FEAT, B, T = x_t.shape
    TAPS, D = tok_w.shape
    CONTEXT = TAPS // FEAT
    L = T - CONTEXT + 1
    HALF = L // 2
    H = 8
    DH = D // H
    NT = -(-L // D)
    LP = NT * D
    LAST = L - (NT - 1) * D
    GH = 4
    E, _, HID = w1.shape
    JH = HID // D
    EPS = 1e-5
    SCALE = DH ** -0.5
    NTOK = B * L
    CAP = (-(-NTOK // D) + 1) * D
    DEAD = E * CAP
    SLOTS = (NTOK + E * (D - 1)) // D + 1
    FAR = 1 << 20
    ROW = 2 * D + 4
    ID, GATE = 2 * D, 2 * D + 1
    Q_PARTS = (0, 0, 1, 1, 0, 2)
    K_PARTS = (0, 1, 0, 1, 2, 0)
    KR = len(Q_PARTS) * DH
    KM = KR + 2
    STEPS = H * 2 * NT
    PASS = NT * GH
    GROUPS = STEPS // GH
    WEIGH_AT = (8, 10, 12, 14, 16, 18, 20, 22, 24, 26, 27, 28)
    N_ST, N_MX, N_P = 2, 3, 3
    CH = 2
    NCH = B // CH

    q_dram = nc.dram_tensor("q_parts_dram", (D, 3, L), bf16).ap()
    k_dram = nc.dram_tensor("k_parts_dram", (D, 3, L), bf16).ap()
    rows_dram = nc.dram_tensor("routed_rows_dram", (DEAD + D, ROW), fp32).ap()
    out_rows = out.rearrange("b t d -> (b t) d")

    ctx = ExitStack()
    with ctx:
        def sb(name, shape, dt=fp32):
            return ctx.enter_context(nc.sbuf_tensor(name, shape, dt))

        def sem(name):
            return ctx.enter_context(nc.semaphore(name))

        seq = sb("seq", [128, B * LP])
        p_ring = sb("p_ring", [128, N_P * GH * HALF])
        patches = p_ring[0:TAPS, 0:N_P * CH * L].rearrange("p (n c t) -> p n c t", n=N_P, c=CH)
        probs = p_ring[:, :].rearrange("p (n j t) -> p n j t", n=N_P, j=GH)
        q_rows = [sb(f"q_rows{n}", [KM, H, LP], bf16) for n in range(2)]
        k_rows = [sb(f"k_rows{n}", [KM, H, L], bf16) for n in range(2)]
        values = [sb(f"values{n}", [128, NT, H, 32]) for n in range(2)]
        q_full, k_full = sb("q_full", [128, L]), sb("k_full", [128, L])
        q_rest, k_rest = sb("q_rest", [128, L]), sb("k_rest", [128, L])
        q_part, k_part = sb("q_part", [128, 3, L], bf16), sb("k_part", [128, 3, L], bf16)
        h_t = sb("h_t", [128, LP])
        h_cur = sb("h_cur", [128, NT, D])
        xn = sb("xn", [128, NT, D])
        xn_t = sb("xn_t", [128, LP])
        o_un = sb("o_un", [128, 2, LP])
        merged = sb("merged", [128, NT, D])
        merged_t = sb("merged_t", [128, LP])
        xn2_t = merged_t
        rows = sb("rows", [128, NT, ROW])
        half_max = sb("half_max", [128, STEPS])
        neg_max = sb("neg_max", [128, STEPS // 2])
        max_parts = sb("max_parts", [128, 2, NT, 2, GH], bf16)
        max_rows = [sb(f"max_rows{g}", [2 * GH, L], bf16) for g in range(2)]
        stats = sb("stats", [128, NT, 6])
        mv = sb("mv", [128, NT, 2])
        var_eps = sb("var_eps", [128, NT])
        rstd = sb("rstd", [128, NT])
        stats2 = sb("stats2", [128, NT, 6])
        mv2 = sb("mv2", [128, NT, 2])
        var_eps2 = sb("var_eps2", [128, NT])
        rstd2 = sb("rstd2", [128, NT])
        r_den = sb("r_den", [128, 4, NT // 2 * GH])
        logits = sb("logits", [128, NT, E])
        top = sb("top", [128, NT])
        scored = sb("scored", [128, NT, E])
        scored2 = sb("scored2", [128, NT, E])
        best = sb("best", [128, NT])
        picked = sb("picked", [128, NT, E])
        onehot = sb("onehot", [128, NT, E], bf16)
        g_diff = sb("g_diff", [128, NT])
        g_exp = sb("g_exp", [128, NT])
        g_inv = sb("g_inv", [128, NT])
        place = sb("place", [128, NT, E])
        place1 = sb("place1", [128, NT, E])
        pos = sb("pos", [128, NT])
        pos_i = sb("pos_i", [128, NT], i32)
        next_row = sb("next_row", [128, E])
        tok_id = sb("tok_id", [128, NT])
        tok_w_sb = sb("tok_w_sb", [TAPS, D])
        wq_sb, wk_sb, wv_sb, wo_sb = (sb(n, [128, D]) for n in ("wq_sb", "wk_sb", "wv_sb", "wo_sb"))
        wr_sb = sb("wr_sb", [128, E])
        tok_b_sb, gamma_sb, beta_sb, bq_sb, bk_sb, bq4 = (
            sb(n, [128, 1]) for n in ("tok_b_sb", "gamma_sb", "beta_sb", "bq_sb", "bk_sb", "bq4"))
        bv_bc, bo_bc, br_bc = sb("bv_bc", [128, D]), sb("bo_bc", [128, D]), sb("br_bc", [128, E])
        bn_stats = sb("bn_stats", [128, 2 * B, 6])
        bn_mv = sb("bn_mv", [128, 2])
        bn_var, bn_rstd, bn_scale, bn_shift, bn_ms = (
            sb(n, [128, 1]) for n in ("bn_var", "bn_rstd", "bn_scale", "bn_shift", "bn_ms"))
        minus_half = sb("minus_half", [128, NT])
        ident, identb = sb("ident", [128, 128]), sb("identb", [128, 128], bf16)
        zero_b = sb("zero_b", [128, NT * E], bf16)
        ones_b, before = sb("ones_b", [128, 128], bf16), sb("before", [128, 128], bf16)
        rank_e = sb("rank_e", [128, NT, E])
        valid = sb("valid", [128, NT, E])
        far = sb("far", [128, NT])
        w1_sb = seq[:, 0:E * HID].rearrange("p (e n) -> p e n", e=E)
        w2_sb = seq[:, E * HID:2 * E * HID].rearrange("p (e n) -> p e n", e=E)
        W_LAST = -(-2 * E * HID // LP)
        b12, b12_rest, b12_rest2 = (t[0:E, 0:HID + D] for t in (xn_t, merged_t, q_rest))
        b12_part = sb("b12_part", [E, 3, HID + D], bf16)
        b12_rows = sb("b12_rows", [128, E, HID + D], bf16)
        pad_row = sb("pad_row", [128, ROW])
        pad_pos, pad_pos_i = sb("pad_pos", [128, E + 1]), sb("pad_pos_i", [128, E + 1], i32)
        region = sb("region", [128, E])
        lane = sb("lane", [128, 1])
        count1, tiles_f, tiles_i = sb("count1", [1, E]), sb("tiles_f", [1, E]), sb("tiles_i", [1, E], i32)
        tiles, cum, skip_e, zero_e = (sb(n, [1, E]) for n in ("tiles", "cum", "skip_e", "zero_e"))
        slot_f = k_part[0:1, :, :].rearrange("p a t -> p (a t)").bitcast(fp32)[:, 0:SLOTS * E]\
            .rearrange("p (s e) -> p s e", e=E)
        beyond = q_part[0:1, :, :].rearrange("p a t -> p (a t)").bitcast(fp32)[:, 0:SLOTS * E]\
            .rearrange("p (s e) -> p s e", e=E)
        beyond_w = o_un[0:1, :, :].rearrange("p a t -> p (a t)")[:, 0:SLOTS * E].rearrange("p (s e) -> p s e", e=E)
        slot_e, slot_r = sb("slot_e", [1, SLOTS]), sb("slot_r", [1, SLOTS])
        slot_e_i, slot_r_i = sb("slot_e_i", [1, SLOTS], i32), sb("slot_r_i", [1, SLOTS], i32)
        def of_ring(first, n):
            return p_ring[:, first:first + n]

        slot_rows = [of_ring(ROW * n, ROW) for n in range(4)]
        slot_xt = [of_ring(4 * ROW + D * n, D) for n in range(2)]
        slot_h = [of_ring(4 * ROW + 2 * D + HID * n, HID) for n in range(2)]
        slot_ht = [of_ring(4 * ROW + 2 * D + HID * (2 + n), HID) for n in range(2)]
        slot_y = [of_ring(4 * ROW + 2 * D + 4 * HID + D * n, D) for n in range(4)]

        psum = ctx.enter_context(nc.psum_tensor("psum", [128, 8, 512], fp32))
        st_bank = [psum[:, n, :] for n in range(N_ST)]
        mx_bank = [psum[:, N_ST + n, :] for n in range(N_MX)]
        o_bank = psum[:, 5, :]
        misc = [psum[:, 6 + n, :] for n in range(2)]
        misc_b = misc[0].bitcast(bf16)

        s_tokw = sem("s_tokw")
        s_const = sem("s_const")
        s_w = sem("s_w")
        s_b12 = sem("s_b12")
        s_patch = [sem(f"s_patch{n}") for n in range(N_P)]
        s_tok = sem("s_tok")
        s_tok_y = sem("s_tok_y")
        s_tok_st = sem("s_tok_st")
        s_bn_pow = sem("s_bn_pow")
        s_pool_c = sem("s_pool_c")
        s_vec_c = sem("s_vec_c")
        s_st = sem("s_st")
        s_exp = sem("s_exp")
        s_pv = sem("s_pv")
        s_o = sem("s_o")
        s_mx = sem("s_mx")
        s_red = sem("s_red")
        s_max = sem("s_max")
        s_misc = sem("s_misc")
        s_free = [sem(f"s_free{n}") for n in range(2)]
        s_ht = sem("s_ht")
        s_ln = sem("s_ln")
        s_ln_p = sem("s_ln_p")
        s_ln2 = sem("s_ln2")
        s_ln2_p = sem("s_ln2_p")
        s_split = sem("s_split")
        s_qk_w = sem("s_qk_w")
        s_ld = [sem(f"s_ld{g}") for g in range(2)]
        s_mrow = sem("s_mrow")
        s_den = sem("s_den")
        s_rt = sem("s_rt")
        s_gate = sem("s_gate")
        s_rk = sem("s_rk")
        s_scat = sem("s_scat")
        s_tab = sem("s_tab")
        s_pad = sem("s_pad")
        s_in = [sem(f"s_in{n}") for n in range(4)]
        s_out = [sem(f"s_out{n}") for n in range(4)]
        s_fx = sem("s_fx")
        s_fxt = sem("s_fxt")
        s_f1 = sem("s_f1")
        s_fr = sem("s_fr")
        s_fh = sem("s_fh")
        s_fht = sem("s_fht")
        s_f2 = sem("s_f2")
        s_fy = sem("s_fy")

        s_apart_v = sem("s_apart_v")
        s_apart_p = sem("s_apart_p")

        FIRST_LOOP, LOOP_PAIRS = 1, (B - 3) // 2
        TASKS = (("MAX1", (1,), ()), ("OT0", (8,), (10,)), ("OT1", (12,), (14,)), ("HTOK", (16,), (18,)),
                 ("V", (20, 21, 22), (24, 25, 26)), ("MT", (28,), (30,)), ("PROJ", (33, 34, 35), (36, 37, 38)),
                 ("XNT", (41,), (43,)), ("Q", (46, 47), (48, 49)), ("MAX0", (51,), ()), ("K", (54, 55), (56, 57)),
                 ("XN2T", (60,), (62,)), ("LOGIT", (65, 66), ()), ("RANK", (78,), (79,)))
        STAGE = {"V": 1, "MAX1": 0, "OT0": -1, "HTOK": 2, "OT1": -1, "MT": -1, "XNT": 2,
                 "PROJ": -1, "Q": 2, "MAX0": 1, "XN2T": -1, "K": 2, "LOGIT": -1, "RANK": -1}

        def live(i, ahead):
            return not isinstance(i, int) or 0 <= i + ahead < B

        def fills(name, bank):
            return sum(bool(at) for n, *banks in TASKS if n == name for at in
                       (banks if bank is None else banks[bank:bank + 1]))

        def fills_before(i, bank):
            def count(n):
                return sum(fills(name, bank) for name in STAGE if 0 <= n + STAGE[name] < B)
            if isinstance(i, int):
                return sum(count(n) for n in range(-2, i))
            return (i - FIRST_LOOP) * sum(fills(name, bank) for name in STAGE) \
                + sum(count(n) for n in range(-2, FIRST_LOOP))

        def fill(i, task, bank):
            k = 0
            for name, *_ in TASKS:
                if name == task:
                    return fills_before(i, None) + (k + 1 + bank)
                k += fills(name, None) if live(i, STAGE[name]) else 0

        def turn_of(i, task, bank):
            k = 0
            for name, *_ in TASKS:
                if name == task:
                    return fills_before(i, bank) + (k + 1)
                k += fills(name, bank) if live(i, STAGE[name]) else 0

        def run_bodies(engine, body):
            for i in range(-2, FIRST_LOOP):
                body(i, i % 2)
            with engine.Fori(0, LOOP_PAIRS) as v:
                for u in range(2):
                    body(v * 2 + (FIRST_LOOP + u), (FIRST_LOOP + u) % 2)
            for i in range(FIRST_LOOP + 2 * LOOP_PAIRS, B + 1):
                body(i, i % 2)

        def wait(engine, semaphore, value):
            if not isinstance(value, int) or value > 0:
                engine.wait_ge(semaphore, value)

        def wait_apart(engine, semaphore, value, counts):
            engine.wait_ge(semaphore, value)
            engine.sem_inc(counts, 1)

        def kn(kt):
            return LAST if kt == NT - 1 else D

        def step_of(s):
            p, kt, j = s // PASS, s % PASS // GH, s % GH
            return p // 2, p % 2, kt, GH * (p // 2) + j, j

        nc.disable_value_cache = True
        block = ctx.enter_context(nc.Block())

        @block.sync
        def _(sp):
            consts = ((tok_w_sb[:, :], tok_w), (tok_b_sb[:, :], tok_b.unsqueeze(1)))
            for dst, src in consts:
                sp.dma_start(dst, src).then_inc(s_tokw, 16)
            for c in range(NCH):
                if c >= N_P:
                    sp.wait_ge(s_tok, 2 * CH * (c - N_P + 1))
                for k in range(CONTEXT):
                    sp.dma_start(patches[FEAT * k:FEAT * (k + 1), c % N_P, :, :],
                                 x_t[:, CH * c:CH * (c + 1), k:k + L]).then_inc(s_patch[c % N_P], 16)
                if c == 0:
                    for dst, src in ((gamma_sb, gamma), (beta_sb, beta), (bq_sb, bq), (bk_sb, bk)):
                        sp.dma_start(dst[:, :], src.unsqueeze(1)).then_inc(s_const, 16)
                    for dst, src in ((bv_bc, bv), (bo_bc, bo), (br_bc, br)):
                        sp.dma_start(dst[:, :], src.partition_broadcast(128)).then_inc(s_const, 16)
                    for dst, src in ((wq_sb, wq), (wk_sb, wk), (wv_sb, wv), (wo_sb, wo), (wr_sb, wr)):
                        sp.dma_start(dst[:, :], src).then_inc(s_const, 16)
                    sp.dma_start(b12[:, 0:HID], b1).then_inc(s_const, 16)
                    sp.dma_start(b12[:, HID:HID + D], b2).then_inc(s_const, 16)
            sp.wait_ge(s_vec_c, 5)
            for n in range(3):
                sp.dma_start(b12_rows[n:n + 1, :, :], b12_part[:, n, :]).then_inc(s_b12, 16)

            def load_group(par, g):
                for dst, src, parts in ((q_rows, q_dram, Q_PARTS), (k_rows, k_dram, K_PARTS)):
                    for n, part in enumerate(parts):
                        sp.dma_start(dst[par][DH * n:DH * (n + 1), GH * g:GH * (g + 1), 0:L],
                                     src[64 * g:64 * (g + 1), part, :].rearrange("(h j) t -> j h t", j=DH))\
                          .then_inc(s_ld[g], 16)

            def body(i, par):
                if live(i, 1):
                    wait(sp, s_st, STEPS * i if live(i, -1) else 0)
                    load_group(1 - par, 1)
                if live(i, 0):
                    sp.wait_ge(s_free[0], turn_of(i, "MAX1", 0))
                    for n in range(2):
                        sp.dma_start(q_rows[par][KR + n:KR + n + 1, GH:H, 0:L],
                                     max_rows[1][GH * n:GH * (n + 1), :]).then_inc(s_mrow, 16)
                if isinstance(i, int) and i == W_LAST + 2:
                    sp.wait_ge(s_ln2, W_LAST * 3 + 1)
                    sp.dma_start(w1_sb[:, :, :], w1.rearrange("e p n -> p e n")).then_inc(s_w, 16)
                    for e in range(E):
                        sp.dma_start(w2_sb[:, e, :].rearrange("p (j n) -> p j n", j=JH),
                                     w2[e].rearrange("(j p) n -> p j n", p=128)).then_inc(s_w, 16)
                if live(i, 2):
                    wait(sp, s_ld[1], (i + 2) * 192)
                    sp.wait_ge(s_split, (i + 2) * 6 + 3)
                    sp.dma_start(q_dram, q_part[:, :, :]).then_inc(s_qk_w, 16)
                    sp.wait_ge(s_split, (i + 2) * 6 + 6)
                    sp.dma_start(k_dram, k_part[:, :, :]).then_inc(s_qk_w, 16)
                if live(i, 1):
                    sp.wait_ge(s_free[0], turn_of(i, "MAX0", 0))
                    for n in range(2):
                        sp.dma_start(q_rows[1 - par][KR + n:KR + n + 1, 0:GH, 0:L],
                                     max_rows[0][GH * n:GH * (n + 1), :]).then_inc(s_mrow, 16)
                if live(i, 2):
                    if live(i, 0):
                        sp.wait_ge(s_st, i * STEPS + STEPS // 2)
                    sp.wait_ge(s_qk_w, (i + 2) * 32 + 32)
                    load_group(par, 0)

            run_bodies(sp, body)

            sp.wait_ge(s_scat, B * NT * 16)
            sp.wait_ge(s_pad, (E + 1) * 16)
            sp.wait_ge(s_tab, 12)

            def load_slot(s, n):
                first = sp.value_load(slot_r_i[0:1, bass.ds(s, 1)], min_val=0, max_val=DEAD)
                sp.dma_start(slot_rows[n][:, :], rows_dram[bass.ds(first, D), :]).then_inc(s_in[n], 16)

            for s in range(4):
                load_slot(s, s)
            with sp.Fori(0, (SLOTS - 6) // 4) as v:
                for u in range(4):
                    sp.wait_ge(s_out[u], v * 16 + 16)
                    load_slot(v * 4 + (4 + u), u)
            done = (SLOTS - 6) // 4
            for s in range(4 + 4 * done, SLOTS):
                sp.wait_ge(s_out[s % 4], 16 * (s // 4))
                load_slot(s, s % 4)
            for n in range(4):
                sp.wait_ge(s_out[n], 16 * len(range(n, SLOTS, 4)))

        @block.gpsimd
        def _(pool):
            nc.gpsimd.memset(ident[:, :], 0.0)
            nc.gpsimd.memset(identb[:, :], 0.0)
            nc.gpsimd.memset(before[:, :], 1.0)
            nc.gpsimd.memset(valid[:, :, :], 1.0)
            nc.gpsimd.memset(far[:, :], 0.0)
            nc.gpsimd.memset(pad_row[:, :], 0.0).then_inc(s_pool_c, 1)
            pool.wait_ge(s_pool_c, 1)
            for m in (ident, identb):
                nc.gpsimd.affine_select(out=m[:, :], in_=m[:, :], compare_op=ALU.not_equal, fill=1.0, base=0,
                                        pattern=[[-1, 128]], channel_multiplier=1)
            nc.gpsimd.affine_select(out=before[:, :], in_=before[:, :], compare_op=ALU.is_gt, fill=0.0, base=0,
                                    pattern=[[1, 128]], channel_multiplier=-1)
            nc.gpsimd.affine_select(out=valid[:, :, :], in_=valid[:, :, :], compare_op=ALU.is_gt, fill=0.0,
                                    base=L, pattern=[[-D, NT], [0, E]], channel_multiplier=-1)
            nc.gpsimd.affine_select(out=far[:, :], in_=far[:, :], compare_op=ALU.is_gt, fill=float(FAR),
                                    base=L, pattern=[[-D, NT]], channel_multiplier=-1)
            nc.gpsimd.iota(tok_id[:, :], [[D, NT]], base=0, channel_multiplier=1,
                           allow_small_or_imprecise_dtypes=True)
            nc.gpsimd.iota(rank_e[:, :, :], [[0, NT], [-1, E]], base=E, channel_multiplier=0,
                           allow_small_or_imprecise_dtypes=True)
            nc.gpsimd.iota(region[:, :], [[CAP, E]], base=0, channel_multiplier=0,
                           allow_small_or_imprecise_dtypes=True)
            nc.gpsimd.iota(next_row[:, :], [[CAP, E]], base=0, channel_multiplier=0,
                           allow_small_or_imprecise_dtypes=True)
            nc.gpsimd.iota(lane[:, :], [[0, 1]], base=0, channel_multiplier=1,
                           allow_small_or_imprecise_dtypes=True)
            nc.gpsimd.iota(pad_row[:, ID:ID + 1].bitcast(i32), [[0, 1]], base=FAR, channel_multiplier=0)\
              .then_inc(s_pool_c, 1)
            pool.wait_ge(s_vec_c, 5)
            pool.wait_ge(s_tok_st, 2 * B + 2)
            nc.gpsimd.tensor_tensor(bn_rstd[:, :], bn_var[:, :], minus_half[:, 0:1], ALU.pow).then_inc(s_bn_pow, 1)

            def split(b, full, rest, part, k):
                nc.gpsimd.tensor_tensor(rest[:, :], full[:, :], part[:, 0, :], ALU.subtract).then_inc(s_split, 1)
                wait_apart(pool, s_split, b * 6 + (k + 1), s_apart_p)
                nc.gpsimd.tensor_scalar(part[:, 1, :], rest[:, :], 1.0, None, ALU.mult).then_inc(s_split, 1)
                pool.wait_ge(s_split, b * 6 + (k + 2))
                nc.gpsimd.tensor_tensor(part[:, 2, :], rest[:, :], part[:, 1, :], ALU.subtract).then_inc(s_split, 1)

            def body(i, par):
                if live(i, 2):
                    b = i + 2
                    pool.wait_ge(s_ln, b * 3 + 3)
                    nc.gpsimd.tensor_tensor(rstd[:, :], var_eps[:, :], minus_half[:, :], ALU.pow).then_inc(s_ln_p, 1)
                    wait_apart(pool, s_ln_p, b * 3 + 1, s_apart_p)
                    for t in range(NT):
                        last = nc.gpsimd.tensor_scalar(xn[:, t, :], h_cur[:, t, :], mv[:, t, 0:1], rstd[:, t:t + 1],
                                                       ALU.subtract, ALU.mult)
                    last.then_inc(s_ln_p, 1)
                    nc.gpsimd.tensor_tensor(seq[:, bass.ds(b * LP, LP)].rearrange("p (t d) -> p t d", t=NT),
                                            h_cur[:, :, :], bo_bc[:, :].unsqueeze(1).to_broadcast([128, NT, D]),
                                            ALU.add).then_inc(s_ln_p, 1)
                if live(i, -1):
                    r = i - 1
                    pool.wait_ge(s_ln2, r * 3 + 3)
                    nc.gpsimd.tensor_tensor(rstd2[:, :], var_eps2[:, :], minus_half[:, :], ALU.pow)\
                      .then_inc(s_ln2_p, 1)
                    wait_apart(pool, s_ln2_p, r * 2 + 1, s_apart_p)
                    for t in range(NT):
                        last = nc.gpsimd.tensor_scalar(rows[:, t, D:2 * D], rows[:, t, 0:D], mv2[:, t, 0:1],
                                                       rstd2[:, t:t + 1], ALU.subtract, ALU.mult)
                    last.then_inc(s_ln2_p, 1)
                if live(i, 2):
                    for bank in range(2):
                        pool.wait_ge(s_free[bank], turn_of(i, "Q", bank))
                    split(b, q_full, q_rest, q_part, 0)
                    for bank in range(2):
                        pool.wait_ge(s_free[bank], turn_of(i, "K", bank))
                    split(b, k_full, k_rest, k_part, 3)
                if live(i, -1):
                    pool.wait_ge(s_rk, r * 4 + 4)
                    wait_apart(pool, s_rt, r * 10 + 10, s_apart_p)
                    for t in range(NT):
                        pool.indirect_dma_start(
                            out=rows_dram, out_offset=bass.IndirectOffsetOnAxis(ap=pos_i[:, t:t + 1], axis=0),
                            in_=rows[:, t, :], in_offset=None, bounds_check=DEAD - 1, oob_is_err=False)\
                            .then_inc(s_scat, 16)

            run_bodies(pool, body)

            nc.gpsimd.iota(slot_f[:, :, :], [[1, SLOTS], [0, E]], base=0, channel_multiplier=0,
                           allow_small_or_imprecise_dtypes=True).then_inc(s_pool_c, 1)
            pool.wait_ge(s_tab, 2)
            for e in range(E + 1):
                pool.indirect_dma_start(
                    out=rows_dram, out_offset=bass.IndirectOffsetOnAxis(ap=pad_pos_i[:, e:e + 1], axis=0),
                    in_=pad_row[:, :], in_offset=None, bounds_check=DEAD + D - 1, oob_is_err=False)\
                    .then_inc(s_pad, 16)

            def store_slot(s, n, s4):
                pool.wait_ge(s_fy, s + 1)
                wait_apart(pool, s_in[n], s4 * 16 + 16, s_apart_p)
                pool.indirect_dma_start(
                    out=out_rows,
                    out_offset=bass.IndirectOffsetOnAxis(ap=slot_rows[n][:, ID:ID + 1].bitcast(i32), axis=0),
                    in_=slot_y[n][:, :], in_offset=None, bounds_check=NTOK - 1, oob_is_err=False)\
                    .then_inc(s_out[n], 16)

            with pool.Fori(0, SLOTS // 4) as v:
                for u in range(4):
                    store_slot(v * 4 + u, u, v)
            for s in range(SLOTS // 4 * 4, SLOTS):
                store_slot(s, s % 4, s // 4)

        @block.scalar
        def _(act):
            act.wait_ge(s_tokw, 16 * 2)
            for n in range(2 * B):
                act.wait_ge(s_tok, n + 1)
                b, half = n // 2, n % 2
                nc.scalar.activation(seq[:, b * LP + half * HALF:b * LP + (half + 1) * HALF],
                                     psum[:, n % 8, 0:HALF], ACT.Relu, bias=tok_b_sb[:, 0:1]).then_inc(s_tok_y, 1)
            act.wait_ge(s_tok_st, 2 * B + 5)
            act.wait_ge(s_vec_c, 5)

            def normed(b, k):
                last = nc.scalar.activation(h_t[:, HALF * k:HALF * (k + 1)], seq[:, bass.ds(b * LP + HALF * k, HALF)],
                                            ACT.Identity, bias=bn_shift[:, 0:1], scale=bn_scale[:, 0:1])
                if k == 1:
                    last.then_inc(s_ht, 1)

            normed(0, 0)
            normed(0, 1)

            def copy_out(i, name, bank, dst):
                act.wait_ge(s_misc, fill(i, name, bank))
                nc.scalar.copy(dst, misc[bank][:, 0:3 * D]).then_inc(s_free[bank], 1)

            def max_out(i, b, g, name):
                act.wait_ge(s_misc, fill(i, name, 0))
                wait(act, s_mrow, (b - 1) * 64 + 32 * (g + 1) if not isinstance(b, int) or b > 0 else 0)
                nc.scalar.copy(max_rows[g][:, :], misc_b[0:2 * GH, 0:L]).then_inc(s_free[0], 1)

            def q_or_k(i, name, bank, k):
                full, part, bias, scale = {"Q": (q_full, q_part, bq4, SCALE), "K": (k_full, k_part, bk_sb, 1.0)}[name]
                dst = (full[:, :] if k == 0 else part[:, 0, :])[:, HALF * bank:HALF * (bank + 1)]
                if k == 0:
                    act.wait_ge(s_misc, fill(i, name, bank))
                    wait(act, s_qk_w, (i + 2) * 32)
                last = nc.scalar.activation(dst, misc[bank][:, 0:HALF], ACT.Identity, bias=bias[:, 0:1], scale=scale)
                if k == 1:
                    last.then_inc(s_free[bank], 1)

            def body(i, par):
                for s in range(STEPS):
                    if live(i, 0):
                        g, qh, kt, h, j = step_of(s)
                        G = s // GH
                        if j == 0:
                            wait(act, s_pv, i * GROUPS + (G - N_P + 1))
                        act.wait_ge(s_st, i * STEPS + (s + 1))
                        nc.scalar.activation(probs[0:kn(kt), G % N_P, j, :], st_bank[s % N_ST][0:kn(kt), 0:HALF],
                                             ACT.Exp).then_inc(s_exp, 1)
                    if s % PASS == 5:
                        b, p = (i, s // PASS - 1) if s >= PASS else (i - 1, 3)
                        if live(i, 0 if s >= PASS else -1):
                            act.wait_ge(s_pv, b * GROUPS + NT * (p + 1))
                            if p < 2 and live(i, -1):
                                act.wait_ge(s_misc, fill(i, f"OT{p}", 1))
                            nc.scalar.copy(o_un[:, p // 2, p % 2 * HALF:(p % 2 + 1) * HALF], o_bank[:, 0:HALF])\
                              .then_inc(s_o, 1)
                    if s == 2 and live(i, 0):
                        max_out(i, i, 1, "MAX1")
                    if s in (17, 19) and live(i, 2):
                        bank = (s - 17) // 2
                        wait(act, s_ln_p, (i + 2) * 3)
                        copy_out(i, "HTOK", bank, h_cur[:, 3 * bank:3 * (bank + 1), :].rearrange("p t d -> p (t d)"))
                    if s in (30, 32) and live(i, -1):
                        bank = (s - 30) // 2
                        copy_out(i, "MT", bank, merged_t[:, 3 * D * bank:3 * D * (bank + 1)])
                    if s in (42, 44) and live(i, 2):
                        bank = (s - 42) // 2
                        copy_out(i, "XNT", bank, xn_t[:, 3 * D * bank:3 * D * (bank + 1)])
                    if 48 <= s < 52 and live(i, 2):
                        q_or_k(i, "Q", (s - 48) // 2, s % 2)
                    if s == 54 and live(i, 1):
                        max_out(i, i + 1, 0, "MAX0")
                    if 56 <= s < 60 and live(i, 2):
                        q_or_k(i, "K", (s - 56) // 2, s % 2)
                    if s in (61, 63) and live(i, -1):
                        bank = (s - 61) // 2
                        copy_out(i, "XN2T", bank, xn2_t[:, 3 * D * bank:3 * D * (bank + 1)])
                    if s == 78 and live(i, -1):
                        act.wait_ge(s_rt, (i - 1) * 10 + 7)
                        nc.scalar.activation(g_exp[:, :], g_diff[:, :], ACT.Exp).then_inc(s_gate, 1)
                    if s in (86, 87) and live(i, 3):
                        if s == 86:
                            act.wait_ge(s_misc, fill(i, "HTOK", 1))
                        normed(i + 3, s - 86)

            run_bodies(act, body)

            def relu(s, n):
                act.wait_ge(s_f1, s + 1)
                if not isinstance(s, int) or s >= 2:
                    act.wait_ge(s_fh, s - 1)
                nc.scalar.activation(slot_h[n % 2][:, :], psum[:, 2 + n % 2, :], ACT.Relu).then_inc(s_fr, 1)

            def xt_evac(s, n):
                act.wait_ge(s_fx, s + 1)
                if not isinstance(s, int) or s >= 2:
                    act.wait_ge(s_f1, s - 1)
                nc.scalar.copy(slot_xt[n % 2][:, :], psum[:, n % 2, 0:D]).then_inc(s_fxt, 1)

            xt_evac(0, 0)
            relu(0, 0)
            xt_evac(1, 1)
            for s in range(1, 5):
                relu(s, s)
                xt_evac(s + 1, s + 1)
            with act.Fori(1, (SLOTS - 2) // 4) as v:
                for u in range(4):
                    relu(v * 4 + (1 + u), 1 + u)
                    xt_evac(v * 4 + (2 + u), 2 + u)
            relu(SLOTS - 1, SLOTS - 1)

        @block.vector
        def _(dve):
            nc.vector.memset(minus_half[:, :], -0.5)
            nc.vector.memset(ones_b[:, :], 1.0)
            nc.vector.memset(zero_b[:, :], 0.0)
            nc.vector.memset(h_t[:, L:LP], 0.0)
            nc.vector.memset(o_un[:, :, L:LP], 1.0)
            nc.vector.memset(rows[:, :, 2 * D:ROW], 0.0)
            nc.vector.memset(zero_e[:, :], 0.0)
            nc.vector.memset(b12_rows[:, :, :], 0.0)
            for n in range(2):
                nc.vector.memset(q_rows[n][0:KR, :, L:LP], 0.0)
                nc.vector.memset(k_rows[n][KR:KM, :, :], 1.0)
                nc.vector.memset(values[n][:, :, :, DH:32], 1.0)
            dve.wait_ge(s_const, 16 * 14)
            nc.vector.tensor_scalar(bq4[:, :], bq_sb[:, :], SCALE, None, ALU.mult)
            nc.vector.tensor_copy(b12_part[:, 0, :], b12[:, :]).then_inc(s_vec_c, 1)
            dve.wait_ge(s_vec_c, 1)
            nc.vector.tensor_tensor(b12_rest[:, :], b12[:, :], b12_part[:, 0, :], ALU.subtract).then_inc(s_vec_c, 1)
            dve.wait_ge(s_vec_c, 2)
            nc.vector.tensor_copy(b12_part[:, 1, :], b12_rest[:, :]).then_inc(s_vec_c, 1)
            dve.wait_ge(s_vec_c, 3)
            nc.vector.tensor_tensor(b12_rest2[:, :], b12_rest[:, :], b12_part[:, 1, :], ALU.subtract)\
              .then_inc(s_vec_c, 1)
            dve.wait_ge(s_vec_c, 4)
            nc.vector.tensor_copy(b12_part[:, 2, :], b12_rest2[:, :]).then_inc(s_vec_c, 1)

            for n in range(2 * B):
                dve.wait_ge(s_tok_y, n + 1)
                b, half = n // 2, n % 2
                nc.vector.bn_stats(bn_stats[:, n, :],
                                   seq[:, b * LP + half * HALF:b * LP + (half + 1) * HALF]).then_inc(s_tok_st, 1)
            dve.wait_ge(s_tok_st, 2 * B)
            nc.vector.bn_aggr(bn_mv[:, :], bn_stats[:, :, :]).then_inc(s_tok_st, 1)
            dve.wait_ge(s_tok_st, 2 * B + 1)
            nc.vector.tensor_scalar(bn_var[:, :], bn_mv[:, 1:2], EPS, None, ALU.add).then_inc(s_tok_st, 1)
            dve.wait_ge(s_bn_pow, 1)
            nc.vector.tensor_tensor(bn_scale[:, :], bn_rstd[:, :], gamma_sb[:, :], ALU.mult).then_inc(s_tok_st, 1)
            dve.wait_ge(s_tok_st, 2 * B + 3)
            nc.vector.tensor_tensor(bn_ms[:, :], bn_mv[:, 0:1], bn_scale[:, :], ALU.mult).then_inc(s_tok_st, 1)
            dve.wait_ge(s_tok_st, 2 * B + 4)
            nc.vector.tensor_tensor(bn_shift[:, :], beta_sb[:, :], bn_ms[:, :], ALU.subtract).then_inc(s_tok_st, 1)
            dve.wait_ge(s_pool_c, 2)

            def layer_stats(b, k, tiles_of, st, mean_var, out_var, counter):
                if k < 3:
                    for t in (2 * k, 2 * k + 1):
                        last = nc.vector.bn_stats(st[:, t, :], tiles_of[:, t, 0:D])
                    if k == 2:
                        last.then_inc(counter, 1)
                elif k < 5:
                    if k == 3:
                        wait_apart(dve, counter, b * 3 + 1, s_apart_v)
                    for t in range(3 * (k - 3), 3 * (k - 2)):
                        last = nc.vector.bn_aggr(mean_var[:, t, :], st[:, t, :])
                    if k == 4:
                        last.then_inc(counter, 1)
                else:
                    dve.wait_ge(counter, b * 3 + 2)
                    nc.vector.tensor_scalar(out_var[:, :], mean_var[:, :, 1], EPS, None, ALU.add)\
                      .then_inc(counter, 1)

            def maxima(b, g):
                k = 3 * g
                dve.wait_ge(s_red, b * STEPS + STEPS // 2 * (g + 1))
                nc.vector.tensor_reduce(neg_max[:, 24 * g:24 * (g + 1)],
                                        half_max[:, 48 * g:48 * (g + 1)].rearrange("p (n a) -> p n a", a=2),
                                        AX.X, ALU.max, negate=True).then_inc(s_max, 1)
                dve.wait_ge(s_max, b * 6 + (k + 1))
                full = neg_max[:, 24 * g:24 * (g + 1)].rearrange("p (h t) -> p t h", h=GH)
                nc.vector.tensor_copy(max_parts[:, g, :, 0, :], full).then_inc(s_max, 1)
                dve.wait_ge(s_max, b * 6 + (k + 2))
                nc.vector.tensor_tensor(max_parts[:, g, :, 1, :], full, max_parts[:, g, :, 0, :], ALU.subtract)\
                  .then_inc(s_max, 1)

            def normalise(i, r, c, bank, k):
                o = misc[bank][:, 0:3 * D].rearrange("p (n c) -> p n c", c=32)
                n = 2 * c + bank
                if k == 0:
                    dve.wait_ge(s_misc, fill(i, f"OT{c}", bank))
                    nc.vector.reciprocal(r_den[:, n, :], o[:, :, DH]).then_inc(s_den, 1)
                else:
                    dve.wait_ge(s_den, r * 4 + (n + 1))
                    nc.vector.tensor_tensor(
                        merged[:, :, :].rearrange("p t (h d) -> p (t h) d", h=H)[:, 12 * n:12 * (n + 1), :],
                        o[:, :, 0:DH], r_den[:, n, :].unsqueeze(2).to_broadcast([128, NT // 2 * GH, DH]), ALU.mult)\
                        .then_inc(s_free[bank], 1)

            def bias_values(i, par, k):
                dve.wait_ge(s_misc, fill(i, "V", k))
                nc.vector.tensor_tensor(
                    values[1 - par][:, 3 * k:3 * (k + 1), :, 0:DH],
                    misc[k][:, 0:3 * D].rearrange("p (t h d) -> p t h d", t=3, h=H),
                    bv_bc[:, :].rearrange("p (h d) -> p h d", h=H).unsqueeze(1).to_broadcast([128, 3, H, DH]), ALU.add)\
                    .then_inc(s_free[k], 1)

            def residual(i, r, k):
                dve.wait_ge(s_misc, fill(i, "PROJ", k))
                if k == 0:
                    dve.wait_ge(s_ln_p, r * 3 + 3)
                    wait(dve, s_scat, r * (NT * 16))
                nc.vector.tensor_tensor(
                    rows[:, 3 * k:3 * (k + 1), 0:D], misc[k][:, 0:3 * D].rearrange("p (t d) -> p t d", t=3),
                    seq[:, bass.ds(r * LP + 3 * D * k, 3 * D)].rearrange("p (t d) -> p t d", t=3), ALU.add)\
                    .then_inc(s_free[k], 1)

            def per(a):
                return a[:, :].unsqueeze(2).to_broadcast([128, NT, E])

            def router(i, r, k):
                if k == 0:
                    dve.wait_ge(s_misc, fill(i, "LOGIT", 0))
                    nc.vector.tensor_tensor(logits[:, :, :], misc[0][:, 0:NT * E].rearrange("p (t e) -> p t e", t=NT),
                                            br_bc[:, :].unsqueeze(1).to_broadcast([128, NT, E]), ALU.add)\
                      .then_inc(s_free[0], 1)
                elif k == 1:
                    dve.wait_ge(s_free[0], turn_of(i, "LOGIT", 0))
                    nc.vector.reduce_max(top[:, :], logits[:, :, :], AX.X).then_inc(s_rt, 1)
                elif k == 2:
                    dve.wait_ge(s_rt, r * 10 + 1)
                    nc.vector.tensor_tensor(scored[:, :, :], logits[:, :, :], per(top), ALU.is_equal)\
                      .then_inc(s_rt, 1)
                elif k == 3:
                    dve.wait_ge(s_rt, r * 10 + 2)
                    nc.vector.tensor_tensor(scored2[:, :, :], scored[:, :, :], rank_e[:, :, :], ALU.mult)\
                      .then_inc(s_rt, 1)
                elif k == 4:
                    dve.wait_ge(s_rt, r * 10 + 3)
                    nc.vector.reduce_max(best[:, :], scored2[:, :, :], AX.X).then_inc(s_rt, 1)
                elif k == 5:
                    dve.wait_ge(s_rt, r * 10 + 4)
                    nc.vector.tensor_tensor(picked[:, :, :], rank_e[:, :, :], per(best), ALU.is_equal)\
                      .then_inc(s_rt, 1)
                elif k == 6:
                    dve.wait_ge(s_rt, r * 10 + 5)
                    nc.vector.tensor_tensor(onehot[:, :, :], picked[:, :, :], valid[:, :, :], ALU.mult)\
                      .then_inc(s_rt, 1)
                elif k == 7:
                    nc.vector.tensor_tensor(g_diff[:, :], top[:, :], top[:, :], ALU.subtract).then_inc(s_rt, 1)
                elif k == 8:
                    dve.wait_ge(s_gate, r + 1)
                    nc.vector.reciprocal(g_inv[:, :], g_exp[:, :]).then_inc(s_rt, 1)
                else:
                    dve.wait_ge(s_rt, r * 10 + 8)
                    nc.vector.tensor_tensor(rows[:, :, GATE], g_exp[:, :], g_inv[:, :], ALU.mult).then_inc(s_rt, 1)

            def ranks(i, r, k):
                if k == 0:
                    dve.wait_ge(s_misc, fill(i, "RANK", 0))
                    nc.vector.tensor_tensor(place[:, :, :], misc[0][:, 0:NT * E].rearrange("p (t e) -> p t e", t=NT),
                                            next_row[:, :].unsqueeze(1).to_broadcast([128, NT, E]), ALU.add)\
                      .then_inc(s_free[0], 1)
                elif k == 1:
                    dve.wait_ge(s_misc, fill(i, "RANK", 1))
                    dve.wait_ge(s_free[0], turn_of(i, "RANK", 0))
                    nc.vector.tensor_tensor(next_row[:, :], misc[1][:, 0:E], next_row[:, :], ALU.add)\
                      .then_inc(s_free[1], 1)
                    nc.vector.tensor_copy(rows[:, :, ID].bitcast(i32), tok_id[:, :]).then_inc(s_rk, 1)
                elif k == 2:
                    nc.vector.tensor_tensor(place1[:, :, :], place[:, :, :], onehot[:, :, :], ALU.mult)\
                      .then_inc(s_rk, 1)
                elif k == 3:
                    dve.wait_ge(s_rk, r * 4 + 2)
                    nc.vector.reduce_sum(pos[:, :], place1[:, :, :], AX.X).then_inc(s_rk, 1)
                elif k == 4:
                    dve.wait_ge(s_rk, r * 4 + 3)
                    nc.vector.tensor_tensor(pos_i[:, :], pos[:, :], far[:, :], ALU.add).then_inc(s_rk, 1)
                else:
                    dve.wait_ge(s_rk, r * 4 + 1)
                    nc.vector.tensor_scalar(tok_id[:, :], tok_id[:, :], float(L), None, ALU.add).then_inc(s_rt, 1)

            def body(i, par):
                for s in range(STEPS):
                    if live(i, 1):
                        dve.wait_ge(s_mx, (i + 1) * STEPS + (s + 1))
                        nc.vector.tensor_reduce(half_max[:, s:s + 1], mx_bank[s % N_MX][:, 0:HALF], AX.X, ALU.max)\
                          .then_inc(s_red, 1)
                        if s % 48 == 47:
                            maxima(i + 1, s // 48)
                    if 9 <= s < 17 and live(i, -1):
                        normalise(i, i - 1, (s - 9) // 4, (s - 9) % 4 // 2, (s - 9) % 2)
                    if 20 <= s < 26 and live(i, 2):
                        if s == 20:
                            for bank in range(2):
                                dve.wait_ge(s_free[bank], turn_of(i, "HTOK", bank))
                        layer_stats(i + 2, s - 20, h_cur, stats, mv, var_eps, s_ln)
                    if s in (26, 27) and live(i, 1):
                        bias_values(i, par, s - 26)
                    if s in (36, 39) and live(i, -1):
                        residual(i, i - 1, s // 39)
                    if 40 <= s < 46 and live(i, -1):
                        if s == 40:
                            for bank in range(2):
                                dve.wait_ge(s_free[bank], turn_of(i, "PROJ", bank))
                        layer_stats(i - 1, s - 40, rows, stats2, mv2, var_eps2, s_ln2)
                    if 68 <= s < 76 and live(i, -1):
                        router(i, i - 1, s - 68)
                    if 80 <= s < 82 and live(i, -1):
                        router(i, i - 1, s - 72)
                    if 82 <= s < 88 and live(i, -1):
                        ranks(i, i - 1, s - 82)

            run_bodies(dve, body)

            dve.wait_ge(s_pool_c, 3)
            nc.vector.tensor_scalar(pad_pos[:, 0:E], next_row[:, :], lane[:, 0:1], None, ALU.add)
            nc.vector.tensor_scalar(pad_pos[:, E:E + 1], lane[:, :], float(DEAD), None, ALU.add).then_inc(s_tab, 1)
            dve.wait_ge(s_tab, 1)
            nc.vector.tensor_copy(pad_pos_i[:, :], pad_pos[:, :]).then_inc(s_tab, 1)
            nc.vector.tensor_tensor(count1[:, :], next_row[0:1, :], region[0:1, :], ALU.subtract).then_inc(s_tab, 1)
            dve.wait_ge(s_tab, 3)
            nc.vector.tensor_scalar(tiles_f[:, :], count1[:, :], 1.0 / D, (D - 1) / D - (D - 1) / (2 * D),
                                    ALU.mult, ALU.add).then_inc(s_tab, 1)
            dve.wait_ge(s_tab, 4)
            nc.vector.tensor_copy(tiles_i[:, :], tiles_f[:, :]).then_inc(s_tab, 1)
            dve.wait_ge(s_tab, 5)
            nc.vector.tensor_copy(tiles[:, :], tiles_i[:, :]).then_inc(s_tab, 1)
            dve.wait_ge(s_tab, 6)
            nc.vector.tensor_tensor_scan(cum[:, :], tiles[:, :], zero_e[:, :], 0.0, ALU.add, ALU.add)
            nc.vector.tensor_scalar(skip_e[:, :], tiles[:, :], -float(D), float(CAP), ALU.mult, ALU.add)\
              .then_inc(s_tab, 1)
            dve.wait_ge(s_tab, 7)
            bc = lambda a: a[:, :].unsqueeze(1).to_broadcast([1, SLOTS, E])
            nc.vector.tensor_tensor(beyond[:, :, :], slot_f[:, :, :], bc(cum), ALU.is_ge).then_inc(s_tab, 1)
            dve.wait_ge(s_tab, 8)
            nc.vector.tensor_tensor(beyond_w[:, :, :], beyond[:, :, :], bc(skip_e), ALU.mult)
            nc.vector.reduce_sum(slot_e[:, :], beyond[:, :, :], AX.X).then_inc(s_tab, 1)
            dve.wait_ge(s_tab, 9)
            nc.vector.reduce_sum(slot_r[:, :], beyond_w[:, :, :], AX.X)
            nc.vector.tensor_scalar(slot_e_i[:, :], slot_e[:, :], float(E - 1), None, ALU.min).then_inc(s_tab, 1)
            dve.wait_ge(s_tab, 10)
            nc.vector.scalar_tensor_tensor(slot_r[:, :], slot_f[:, :, 0], float(D), slot_r[:, :], ALU.mult, ALU.add)\
              .then_inc(s_tab, 1)
            dve.wait_ge(s_tab, 11)
            nc.vector.tensor_scalar(slot_r_i[:, :], slot_r[:, :], float(DEAD), None, ALU.min).then_inc(s_tab, 1)

            def ht_evac(s, n):
                dve.wait_ge(s_fh, s + 1)
                if not isinstance(s, int) or s >= 2:
                    dve.wait_ge(s_f2, s - 1)
                nc.vector.tensor_copy(slot_ht[n % 2][:, :], psum[:, 4 + n % 2, :]).then_inc(s_fht, 1)

            def result(s, n, s4):
                dve.wait_ge(s_f2, s + 1)
                dve.wait_ge(s_in[n % 4], s4 * 16 + 16)
                if not isinstance(s4, int) or s4 > 0:
                    dve.wait_ge(s_out[n % 4], s4 * 16)
                nc.vector.scalar_tensor_tensor(slot_y[n % 4][:, :], psum[:, 6 + n % 2, 0:D],
                                               slot_rows[n % 4][:, GATE:GATE + 1], slot_rows[n % 4][:, 0:D],
                                               ALU.mult, ALU.add).then_inc(s_fy, 1)

            for s in range(4):
                ht_evac(s, s)
                result(s, s, 0)
            with dve.Fori(1, SLOTS // 4) as v:
                for u in range(4):
                    ht_evac(v * 4 + u, u)
                    result(v * 4 + u, u, v)
            for s in range(SLOTS // 4 * 4, SLOTS):
                ht_evac(s, s)
                result(s, s, s // 4)

        @block.tensor
        def _(pe):
            pe.wait_ge(s_tokw, 16 * 2)
            for n in range(2 * B):
                c, b, half = n // (2 * CH), n // 2, n % 2
                if n % (2 * CH) == 0:
                    pe.wait_ge(s_patch[c % N_P], 16 * CONTEXT * (c // N_P + 1))
                if n >= 8:
                    pe.wait_ge(s_tok_y, n - 7)
                nc.tensor.matmul(psum[:, n % 8, 0:HALF], tok_w_sb[:, :],
                                 patches[:, c % N_P, b % CH, half * HALF:(half + 1) * HALF],
                                 start=True, stop=True).then_inc(s_tok, 1)
            pe.wait_ge(s_tok_y, 2 * B)
            pe.wait_ge(s_pool_c, 2)
            pe.wait_ge(s_vec_c, 5)
            pe.wait_ge(s_const, 16 * 14)
            pe.wait_ge(s_b12, 16 * 3)

            def transposes(bank, src):
                for n in range(3):
                    last = nc.tensor.transpose(misc[bank][:, D * n:D * (n + 1)], src(3 * bank + n), ident[:, :])
                return last

            def task(i, par, name, bank, k, pieces):
                if k == 0:
                    wait(pe, s_free[bank], turn_of(i, name, bank) - 1)
                if name == "V":
                    t = 3 * bank + k
                    last = nc.tensor.matmul(misc[bank][:, D * k:D * (k + 1)], xn_t[:, D * t:D * (t + 1)], wv_sb[:, :],
                                            start=True, stop=True)
                elif name in ("MAX0", "MAX1"):
                    g = int(name[3])
                    pe.wait_ge(s_max, (i + (1 - g)) * 6 + 3 * (g + 1))
                    for t in range(NT):
                        last = nc.tensor.transpose(misc_b[0:2 * GH, D * t:D * (t + 1)],
                                                   max_parts[:, g, t, :, :].rearrange("p a h -> p (a h)"), identb[:, :])
                elif name in ("OT0", "OT1"):
                    pe.wait_ge(s_o, (i - 1) * 4 + 4)
                    t0 = 3 * int(name[2])
                    last = transposes(bank, lambda n: o_un[:, n % 2, D * (t0 + n // 2):D * (t0 + n // 2 + 1)])
                elif name == "HTOK":
                    pe.wait_ge(s_ht, (i + 2) + 1)
                    last = transposes(bank, lambda t: h_t[:, D * t:D * (t + 1)])
                elif name == "MT":
                    pe.wait_ge(s_free[1], turn_of(i, f"OT{bank}", 1))
                    last = transposes(bank, lambda t: merged[:, t, :])
                elif name == "XNT":
                    pe.wait_ge(s_ln_p, (i + 2) * 3 + 2)
                    last = transposes(bank, lambda t: xn[:, t, :])
                elif name == "PROJ":
                    t = 3 * bank + k
                    last = nc.tensor.matmul(misc[bank][:, D * k:D * (k + 1)], merged_t[:, D * t:D * (t + 1)],
                                            wo_sb[:, :], start=True, stop=True)
                elif name in ("Q", "K"):
                    first, n = (0, HALF // 2) if k == 0 else (HALF // 2, HALF - HALF // 2)
                    last = nc.tensor.matmul(misc[bank][:, first:first + n], (wq_sb if name == "Q" else wk_sb)[:, :],
                                            xn_t[:, bank * HALF + first:bank * HALF + first + n],
                                            start=True, stop=True)
                elif name == "XN2T":
                    pe.wait_ge(s_ln2_p, (i - 1) * 2 + 2)
                    last = transposes(bank, lambda t: rows[:, t, D:2 * D])
                elif name == "LOGIT":
                    if k == 0:
                        pe.wait_ge(s_free[1], turn_of(i, "XN2T", 1))
                    for t in range(3 * k, 3 * (k + 1)):
                        last = nc.tensor.matmul(misc[0][:, E * t:E * (t + 1)], xn2_t[:, D * t:D * (t + 1)],
                                                wr_sb[:, :], start=True, stop=True)
                elif bank == 0:
                    pe.wait_ge(s_rt, (i - 1) * 10 + 6)
                    nc.tensor.matmul(misc[0][:, 0:NT * E], before[:, :],
                                     onehot[:, :, :].rearrange("p t e -> p (t e)"), start=True, stop=False)
                    for t in range(NT - 1):
                        nc.tensor.matmul(misc[0][:, E * (t + 1):NT * E].rearrange("p (t e) -> p t e", e=E),
                                         ones_b[:, :], onehot[:, t:t + 1, :].to_broadcast([128, NT - 1 - t, E]),
                                         start=False, stop=False)
                    last = nc.tensor.matmul(misc[0][:, 0:NT * E], ones_b[:, :], zero_b[:, :], start=False, stop=True)
                else:
                    for t in range(NT):
                        last = nc.tensor.matmul(misc[1][:, 0:E], ones_b[:, :], onehot[:, t, :],
                                                start=t == 0, stop=t == NT - 1)
                if k == pieces - 1:
                    last.then_inc(s_misc, 1)

            def weigh(b, par, G, k):
                p, kt = G // NT, G % NT
                first, n = (0, HALF // 2) if k == 0 else (HALF // 2, HALF - HALF // 2)
                if k == 0:
                    pe.wait_ge(s_exp, b * STEPS + GH * (G + 1))
                    if kt == 0:
                        wait(pe, s_o, b * 4 + p)
                for j in range(GH):
                    last = nc.tensor.matmul(o_bank[32 * j:32 * (j + 1), first:first + n],
                                            values[par][0:kn(kt), kt, GH * (p // 2) + j, :],
                                            probs[0:kn(kt), G % N_P, j, first:first + n],
                                            start=kt == 0 and k == 0, stop=kt == NT - 1, skip_group_check=True)
                if k == 1:
                    last.then_inc(s_pv, 1)

            def body(i, par):
                for s in range(STEPS):
                    if live(i, 0):
                        g, qh, kt, h, j = step_of(s)
                        if s % 48 == 0:
                            pe.wait_ge(s_mrow, i * 64 + 32 * (g + 1))
                        wait(pe, s_exp, i * STEPS + (s + 1 - N_ST))
                        nc.tensor.matmul(st_bank[s % N_ST][0:kn(kt), 0:HALF],
                                         k_rows[par][0:KM, h, D * kt:D * kt + kn(kt)],
                                         q_rows[par][0:KM, h, qh * HALF:(qh + 1) * HALF],
                                         start=True, stop=True).then_inc(s_st, 1)
                    if live(i, 1):
                        b, h, t, half = i + 1, s // 12, s % 12 // 2, s % 2
                        if s % 48 == 0:
                            pe.wait_ge(s_ld[s // 48], b * 192 + 192)
                        wait(pe, s_red, b * STEPS + (s + 1 - N_MX))
                        nc.tensor.matmul(mx_bank[s % N_MX][:, 0:HALF], q_rows[1 - par][0:KR, h, D * t:D * (t + 1)],
                                         k_rows[1 - par][0:KR, h, half * HALF:(half + 1) * HALF],
                                         start=True, stop=True).then_inc(s_mx, 1)
                    for n, after in enumerate(WEIGH_AT):
                        p = (s - after) // PASS
                        if (s - after) % PASS == 0 and live(i, 0 if p >= 0 else -1):
                            weigh(i if p >= 0 else i - 1, par if p >= 0 else 1 - par, p % 4 * NT + n // 2, n % 2)
                    for name, *banks in TASKS:
                        for bank, at in enumerate(banks):
                            if s in at and live(i, STAGE[name]):
                                task(i, par, name, bank, at.index(s), len(at))

            run_bodies(pe, body)

            pe.wait_ge(s_tab, 12)
            pe.wait_ge(s_w, 16 * (E + 1))

            def x_t_slot(s, n, s4):
                pe.wait_ge(s_in[n % 4], s4 * 16 + 16)
                if not isinstance(s, int) or s >= 2:
                    pe.wait_ge(s_fxt, s - 1)
                nc.tensor.transpose(psum[:, n % 2, 0:D], slot_rows[n % 4][:, D:2 * D], ident[:, :]).then_inc(s_fx, 1)

            def layer1(s, n):
                e = pe.value_load(slot_e_i[0:1, bass.ds(s, 1)], min_val=0, max_val=E - 1)
                pe.wait_ge(s_fxt, s + 1)
                if not isinstance(s, int) or s >= 2:
                    pe.wait_ge(s_fr, s - 1)
                nc.tensor.matmul(psum[:, 2 + n % 2, :], slot_xt[n % 2][:, :], w1_sb[:, bass.ds(e, 1), :],
                                 start=True, stop=False)
                nc.tensor.matmul(psum[:, 2 + n % 2, :], ones_b[:, :], b12_rows[:, bass.ds(e, 1), 0:HID],
                                 start=False, stop=True).then_inc(s_f1, 1)

            def h_t_slot(s, n):
                pe.wait_ge(s_fr, s + 1)
                if not isinstance(s, int) or s >= 2:
                    pe.wait_ge(s_fht, s - 1)
                for k in range(JH):
                    last = nc.tensor.transpose(psum[:, 4 + n % 2, D * k:D * (k + 1)],
                                               slot_h[n % 2][:, D * k:D * (k + 1)], ident[:, :])
                last.then_inc(s_fh, 1)

            def layer2(s, n):
                e = pe.value_load(slot_e_i[0:1, bass.ds(s, 1)], min_val=0, max_val=E - 1)
                pe.wait_ge(s_fht, s + 1)
                if not isinstance(s, int) or s >= 2:
                    pe.wait_ge(s_fy, s - 1)
                for k in range(JH):
                    nc.tensor.matmul(psum[:, 6 + n % 2, 0:D], slot_ht[n % 2][:, D * k:D * (k + 1)],
                                     w2_sb[:, bass.ds(e, 1), D * k:D * (k + 1)], start=k == 0, stop=False)
                nc.tensor.matmul(psum[:, 6 + n % 2, 0:D], ones_b[:, :], b12_rows[:, bass.ds(e, 1), HID:HID + D],
                                 start=False, stop=True).then_inc(s_f2, 1)

            x_t_slot(0, 0, 0)
            layer1(0, 0)
            x_t_slot(1, 1, 0)

            def turn(v, u):
                h_t_slot(v * 4 + u, u)
                layer1(v * 4 + (1 + u), 1 + u)
                layer2(v * 4 + u, u)
                x_t_slot(v * 4 + (2 + u), 2 + u, v + (2 + u) // 4)

            for u in range(4):
                turn(0, u)
            with pe.Fori(1, (SLOTS - 2) // 4) as v:
                for u in range(4):
                    turn(v, u)
            h_t_slot(SLOTS - 2, SLOTS - 2)
            layer1(SLOTS - 1, SLOTS - 1)
            layer2(SLOTS - 2, SLOTS - 2)
            h_t_slot(SLOTS - 1, SLOTS - 1)
            layer2(SLOTS - 1, SLOTS - 1)


def kernel(**inputs):
    import numpy as np
    import concourse.bacc as bacc
    from concourse.bass_utils import run_bass_kernel_spmd

    def a(name):
        return np.asarray(inputs[name])

    arrays = {
        "x_t": a("x").transpose(2, 0, 1),
        "tok_w": a("L0_tok_W").T, "tok_b": a("L0_tok_b"), "gamma": a("L0_tok_gamma"), "beta": a("L0_tok_beta"),
        "wq": a("L0_attn_Wq").T, "bq": a("L0_attn_bq"), "wk": a("L0_attn_Wk").T, "bk": a("L0_attn_bk"),
        "wv": a("L0_attn_Wv").T, "bv": a("L0_attn_bv"), "wo": a("L0_attn_Wo").T, "bo": a("L0_attn_bo"),
        "wr": a("L0_ffn_Wr"), "br": a("L0_ffn_br"), "w1": a("L0_ffn_W1"), "b1": a("L0_ffn_b1"),
        "w2": a("L0_ffn_W2"), "b2": a("L0_ffn_b2"),
    }
    arrays = {f"in_{n}_dram": np.ascontiguousarray(v) for n, v in arrays.items()}
    nc = bacc.Bacc("TRN2", target_bir_lowering=False, num_devices=1)
    args = [nc.dram_tensor(n, v.shape, mybir.dt.from_np(v.dtype), kind="ExternalInput").ap()
            for n, v in arrays.items()]
    b, frames, feat = inputs["x"].shape
    channels, taps = inputs["L0_tok_W"].shape
    shape = (b, frames - taps // feat + 1, channels)
    args.append(nc.dram_tensor("out_dram", shape, mybir.dt.float32, kind="ExternalOutput").ap())
    audio_tower(nc, *args)
    return run_bass_kernel_spmd(nc, [arrays], core_ids=[0]).results[0]["out_dram"]
```

```python
import concourse.bass as bass
from concourse import mybir
from contextlib import ExitStack


def audio_tower(
    nc: bass.Bass,
    x_t: bass.AP,
    tok_w: bass.AP,
    tok_b: bass.AP,
    gamma: bass.AP,
    beta: bass.AP,
    wq: bass.AP,
    bq: bass.AP,
    wk: bass.AP,
    bk: bass.AP,
    wv: bass.AP,
    bv: bass.AP,
    wo: bass.AP,
    bo: bass.AP,
    wr: bass.AP,
    br: bass.AP,
    w1: bass.AP,
    b1: bass.AP,
    w2: bass.AP,
    b2: bass.AP,
    out: bass.AP,
):
    fp32 = mybir.dt.float32
    bf16 = mybir.dt.bfloat16
    i32 = mybir.dt.int32
    ALU = mybir.AluOpType
    ACT = mybir.ActivationFunctionType
    AX = mybir.AxisListType

    FEAT, B, T = x_t.shape
    TAPS, D = tok_w.shape
    CONTEXT = TAPS // FEAT
    L = T - CONTEXT + 1
    HALF = L // 2
    H = 8
    DH = D // H
    NT = -(-L // D)
    LP = NT * D
    LAST = L - (NT - 1) * D
    GH = 4
    E, _, HID = w1.shape
    JH = HID // D
    EPS = 1e-5
    SCALE = DH ** -0.5
    NTOK = B * L
    CAP = (-(-NTOK // D) + 1) * D
    DEAD = E * CAP
    SLOTS = (NTOK + E * (D - 1)) // D + 1
    ROUND = 6
    assert SLOTS <= 128
    FAR = 1 << 20
    ROW = 2 * D + 4
    ID, GATE = 2 * D, 2 * D + 1
    Q_PARTS = (0, 0, 1, 1, 0, 2)
    K_PARTS = (0, 1, 0, 1, 2, 0)
    KR = len(Q_PARTS) * DH
    KM = KR + 2
    STEPS = H * 2 * NT
    PASS = NT * GH
    GROUPS = STEPS // GH
    PARTS = 2
    WEIGH_AT = (7, 9, 11, 13, 15, 17, 19, 21, 23, 25, 27, 28)
    OUT_AT = 5
    N_ST, N_MX, N_P = 2, 3, 3
    CH = 2
    NCH = B // CH

    q_dram = nc.dram_tensor("q_parts_dram", (D, 3, L), bf16).ap()
    k_dram = nc.dram_tensor("k_parts_dram", (D, 3, L), bf16).ap()
    rows_dram = nc.dram_tensor("routed_rows_dram", (DEAD + D, ROW), fp32).ap()
    out_rows = out.rearrange("b t d -> (b t) d")

    ctx = ExitStack()
    with ctx:
        def sb(name, shape, dt=fp32):
            return ctx.enter_context(nc.sbuf_tensor(name, shape, dt))

        def sem(name):
            return ctx.enter_context(nc.semaphore(name))

        seq = sb("seq", [128, B * LP])
        p_ring = sb("p_ring", [128, N_P * GH * HALF])
        patches = p_ring[0:TAPS, 0:N_P * CH * L].rearrange("p (n c t) -> p n c t", n=N_P, c=CH)
        probs = p_ring[:, :].rearrange("p (n j t) -> p n j t", n=N_P, j=GH)
        q_rows = [sb(f"q_rows{n}", [KM, H, LP], bf16) for n in range(2)]
        k_rows = [sb(f"k_rows{n}", [KM, H, L], bf16) for n in range(2)]
        values = [sb(f"values{n}", [128, NT, H, 32]) for n in range(2)]
        q_full, k_full = sb("q_full", [128, L]), sb("k_full", [128, L])
        q_rest, k_rest = sb("q_rest", [128, L]), sb("k_rest", [128, L])
        q_part, k_part = sb("q_part", [128, 3, L], bf16), sb("k_part", [128, 3, L], bf16)
        h_t = sb("h_t", [128, LP])
        h_cur = sb("h_cur", [128, NT, D])
        xn = sb("xn", [128, NT, D])
        xn_t = sb("xn_t", [128, LP])
        o_un = sb("o_un", [128, 2, LP])
        merged = sb("merged", [128, NT, D])
        merged_t = sb("merged_t", [128, LP])
        xn2_t = merged_t
        rows = sb("rows", [128, NT, ROW])
        half_max = sb("half_max", [128, STEPS])
        neg_max = sb("neg_max", [128, STEPS // 2])
        max_parts = sb("max_parts", [128, 2, NT, 2, GH], bf16)
        max_rows = [sb(f"max_rows{g}", [2 * GH, L], bf16) for g in range(2)]
        stats = sb("stats", [128, NT, 6])
        mv = sb("mv", [128, NT, 2])
        var_eps = sb("var_eps", [128, NT])
        rstd = sb("rstd", [128, NT])
        stats2 = sb("stats2", [128, NT, 6])
        mv2 = sb("mv2", [128, NT, 2])
        var_eps2 = sb("var_eps2", [128, NT])
        rstd2 = sb("rstd2", [128, NT])
        r_den = sb("r_den", [128, 4, NT // 2 * GH])
        logits = sb("logits", [128, NT, E])
        top = sb("top", [128, NT])
        scored = sb("scored", [128, NT, E])
        scored2 = sb("scored2", [128, NT, E])
        best = sb("best", [128, NT])
        picked = sb("picked", [128, NT, E])
        onehot = sb("onehot", [128, NT + 1, E], bf16)
        g_diff = sb("g_diff", [128, NT])
        g_exp = sb("g_exp", [128, NT])
        g_inv = sb("g_inv", [128, NT])
        place = sb("place", [128, NT, E])
        place1 = sb("place1", [128, NT, E])
        pos = sb("pos", [128, NT])
        pos_i = sb("pos_i", [128, NT], i32)
        next_row = sb("next_row", [128, E])
        tok_id = sb("tok_id", [128, NT])
        tok_w_sb = sb("tok_w_sb", [TAPS, D])
        wq_sb, wk_sb, wv_sb, wo_sb = (sb(n, [128, D]) for n in ("wq_sb", "wk_sb", "wv_sb", "wo_sb"))
        wr_sb = sb("wr_sb", [128, E])
        tok_b_sb, gamma_sb, beta_sb, bq_sb, bk_sb, bq4 = (
            sb(n, [128, 1]) for n in ("tok_b_sb", "gamma_sb", "beta_sb", "bq_sb", "bk_sb", "bq4"))
        bv_bc, bo_bc, br_bc = sb("bv_bc", [128, D]), sb("bo_bc", [128, D]), sb("br_bc", [128, E])
        bn_stats = sb("bn_stats", [128, 2 * B, 6])
        bn_mv = sb("bn_mv", [128, 2])
        bn_var, bn_rstd, bn_scale, bn_shift, bn_ms = (
            sb(n, [128, 1]) for n in ("bn_var", "bn_rstd", "bn_scale", "bn_shift", "bn_ms"))
        minus_half = sb("minus_half", [128, NT])
        ident, identb = sb("ident", [128, 128]), sb("identb", [128, 128], bf16)
        zero_b = sb("zero_b", [128, (NT + 1) * E], bf16)
        ones_b, before = sb("ones_b", [128, 128], bf16), sb("before", [128, 128], bf16)
        rank_e = sb("rank_e", [128, NT, E])
        valid = sb("valid", [128, NT, E])
        far = sb("far", [128, NT])
        W1, W2, B2, B1 = 0, HID, 2 * HID, 2 * HID + D
        W_ALL = B1 + JH
        w_sb = seq[:, 0:E * W_ALL].rearrange("p (e n) -> p e n", e=E)
        W_LAST = -(-E * W_ALL // LP)
        pad_row = sb("pad_row", [128, ROW])
        pad_i = sb("pad_i", [1, E], i32)
        region = sb("region", [128, E])
        lane = sb("lane", [128, 1])
        tiles_i = sb("tiles_i", [128, E], i32)
        count, tiles_f, tiles, cum, skip_e, zero_e, beyond, beyond_w = (sb(n, [128, E]) for n in (
            "count", "tiles_f", "tiles", "cum", "skip_e", "zero_e", "beyond", "beyond_w"))
        slot_e, slot_r, slot_r0 = sb("slot_e", [128, 1]), sb("slot_r", [128, 1]), sb("slot_r0", [128, 1])
        slot_e_i, slot_r_i = sb("slot_e_i", [1, 128], i32), sb("slot_r_i", [1, 128], i32)

        def of_ring(first, n):
            return p_ring[:, first:first + n]

        slot_rows = [of_ring(ROW * n, ROW) for n in range(ROUND)]
        slot_y = [of_ring(ROUND * ROW + D * n, D) for n in range(ROUND)]
        slot_xt = [of_ring(ROUND * (ROW + D) + D * n, D) for n in range(2)]
        slot_ht = [of_ring(ROUND * (ROW + D) + 2 * D + HID * n, HID) for n in range(2)]
        slot_w = [seq[:, W_ALL * n:W_ALL * (n + 1)] for n in (E, E + 1)] + [sb("slot_w2", [128, W_ALL])[:, :]]
        slot_id = sb("slot_id", [128, ROUND], i32)
        N_W = len(slot_w)

        psum = ctx.enter_context(nc.psum_tensor("psum", [128, 8, 512], fp32))
        st_bank = [psum[:, n, :] for n in range(N_ST)]
        mx_bank = [psum[:, N_ST + n, :] for n in range(N_MX)]
        o_bank = psum[:, 5, :]
        misc = [psum[:, 6 + n, :] for n in range(2)]
        misc_b = misc[0].bitcast(bf16)

        s_tokw = sem("s_tokw")
        s_const = sem("s_const")
        s_w = sem("s_w")
        s_patch = [sem(f"s_patch{n}") for n in range(N_P)]
        s_tok = sem("s_tok")
        s_tok_y = sem("s_tok_y")
        s_tok_st = sem("s_tok_st")
        s_bn_pow = sem("s_bn_pow")
        s_pool_c = sem("s_pool_c")
        s_vec_c = sem("s_vec_c")
        s_st = sem("s_st")
        s_exp = sem("s_exp")
        s_pv = sem("s_pv")
        s_o = sem("s_o")
        s_mx = sem("s_mx")
        s_red = sem("s_red")
        s_max = sem("s_max")
        s_misc = sem("s_misc")
        s_free = [sem(f"s_free{n}") for n in range(2)]
        s_ht = sem("s_ht")
        s_ln = sem("s_ln")
        s_ln_p = sem("s_ln_p")
        s_ln2 = sem("s_ln2")
        s_ln2_p = sem("s_ln2_p")
        s_split = sem("s_split")
        s_qk_w = sem("s_qk_w")
        s_ld = [sem(f"s_ld{g}") for g in range(2)]
        s_mrow = sem("s_mrow")
        s_den = sem("s_den")
        s_rt = sem("s_rt")
        s_gate = sem("s_gate")
        s_rk = sem("s_rk")
        s_scat = sem("s_scat")
        s_tab = sem("s_tab")
        s_tab_t = sem("s_tab_t")
        s_pad = sem("s_pad")
        s_in = [sem(f"s_in{n}") for n in range(ROUND)]
        s_out = [sem(f"s_out{n}") for n in range(ROUND)]
        s_fx = sem("s_fx")
        s_fxt = sem("s_fxt")
        s_f1 = sem("s_f1")
        s_fr = sem("s_fr")
        s_fw = sem("s_fw")
        s_f2 = sem("s_f2")
        s_fb = sem("s_fb")
        s_fy = sem("s_fy")

        s_apart_v = sem("s_apart_v")
        s_apart_p = sem("s_apart_p")

        FIRST_LOOP, LOOP_PAIRS = 1, (B - 3) // 2
        TASKS = (("MAX1", (2,), ()), ("OT0", (8,), (10,)), ("OT1", (12,), (14,)), ("HTOK", (16,), (18,)),
                 ("V", (20, 21, 22), (24, 25, 26)), ("MT", (28,), (30,)), ("PROJ", (33, 34, 35), (36, 37, 38)),
                 ("XNT", (40,), (42,)), ("Q", (46, 47), (48, 49)), ("MAX0", (51,), ()), ("K", (57, 58), (59, 60)),
                 ("XN2T", (64,), (66,)), ("LOGIT", (70, 72), ()), ("RANK", (84,), ()))
        STAGE = {"V": 1, "MAX1": 0, "OT0": -1, "HTOK": 2, "OT1": -1, "MT": -1, "XNT": 2,
                 "PROJ": -1, "Q": 2, "MAX0": 1, "XN2T": -1, "K": 2, "LOGIT": -1, "RANK": -1}

        def live(i, ahead):
            return not isinstance(i, int) or 0 <= i + ahead < B

        def fills(name, bank):
            return sum(bool(at) for n, *banks in TASKS if n == name for at in
                       (banks if bank is None else banks[bank:bank + 1]))

        def fills_before(i, bank):
            def count(n):
                return sum(fills(name, bank) for name in STAGE if 0 <= n + STAGE[name] < B)
            if isinstance(i, int):
                return sum(count(n) for n in range(-2, i))
            return (i - FIRST_LOOP) * sum(fills(name, bank) for name in STAGE) \
                + sum(count(n) for n in range(-2, FIRST_LOOP))

        def fill(i, task, bank):
            k = 0
            for name, *_ in TASKS:
                if name == task:
                    return fills_before(i, None) + (k + 1 + bank)
                k += fills(name, None) if live(i, STAGE[name]) else 0

        def turn_of(i, task, bank):
            k = 0
            for name, *_ in TASKS:
                if name == task:
                    return fills_before(i, bank) + (k + 1)
                k += fills(name, bank) if live(i, STAGE[name]) else 0

        def run_bodies(engine, body):
            for i in range(-2, FIRST_LOOP):
                body(i, i % 2)
            with engine.Fori(0, LOOP_PAIRS) as v:
                for u in range(2):
                    body(v * 2 + (FIRST_LOOP + u), (FIRST_LOOP + u) % 2)
            for i in range(FIRST_LOOP + 2 * LOOP_PAIRS, B + 1):
                body(i, i % 2)

        def run_slots(engine, ahead, turn):
            for s in range(ROUND):
                turn(s, s, 0)
            rounds = (SLOTS - ahead) // ROUND
            with engine.Fori(1, rounds) as v:
                for u in range(ROUND):
                    turn(v * ROUND + u, u, v)
            for s in range(rounds * ROUND, SLOTS):
                turn(s, s % ROUND, s // ROUND)

        TABLES = 11

        def later(s, n, r, k):
            return s + k, (n + k) % ROUND, r + (n + k) // ROUND

        FIRST_BODY, LAST_BODY = -2, B

        def is_body(i, number):
            return isinstance(i, int) and i == number

        def norm_rows(ops, dst, src, mean_var, r_root, counter):
            for t in range(NT):
                last = ops.tensor_scalar(dst(t), src(t), mean_var[:, t, 0:1], r_root[:, t:t + 1],
                                         ALU.subtract, ALU.mult)
            last.then_inc(counter, 1)

        def split(engine, ops, counts, i, name):
            full, rest, part, k = {"Q": (q_full, q_rest, q_part, 0), "K": (k_full, k_rest, k_part, 3)}[name]
            done = (i + 2) * 6 + k
            for bank in range(2):
                engine.wait_ge(s_free[bank], turn_of(i, name, bank))
            ops.tensor_tensor(rest[:, :], full[:, :], part[:, 0, :], ALU.subtract).then_inc(s_split, 1)
            wait_apart(engine, s_split, done + 1, counts)
            ops.tensor_scalar(part[:, 1, :], rest[:, :], 1.0, None, ALU.mult).then_inc(s_split, 1)
            engine.wait_ge(s_split, done + 2)
            ops.tensor_tensor(part[:, 2, :], rest[:, :], part[:, 1, :], ALU.subtract).then_inc(s_split, 1)

        def pad_regions(engine, experts):
            engine.wait_ge(s_tab, 1)
            for e in experts:
                first = engine.value_load(pad_i[0:1, e:e + 1], min_val=0, max_val=DEAD - D)
                engine.dma_start(rows_dram[bass.ds(first, D), :], pad_row[:, :]).then_inc(s_pad, 16)

        def wait(engine, semaphore, value):
            if not isinstance(value, int) or value > 0:
                engine.wait_ge(semaphore, value)

        def wait_apart(engine, semaphore, value, counts):
            engine.wait_ge(semaphore, value)
            engine.sem_inc(counts, 1)

        def kn(kt):
            return LAST if kt == NT - 1 else D

        def step_of(s):
            p, kt, j = s // PASS, s % PASS // GH, s % GH
            return p // 2, p % 2, kt, GH * (p // 2) + j, j

        nc.disable_value_cache = True
        block = ctx.enter_context(nc.Block())

        @block.sync
        def _(sp):
            consts = ((tok_w_sb[:, :], tok_w), (tok_b_sb[:, :], tok_b.unsqueeze(1)))
            for dst, src in consts:
                sp.dma_start(dst, src).then_inc(s_tokw, 16)
            for c in range(NCH):
                if c >= N_P:
                    sp.wait_ge(s_tok, 2 * CH * (c - N_P + 1))
                for k in range(CONTEXT):
                    sp.dma_start(patches[FEAT * k:FEAT * (k + 1), c % N_P, :, :],
                                 x_t[:, CH * c:CH * (c + 1), k:k + L]).then_inc(s_patch[c % N_P], 16)
                if c == 0:
                    for dst, src in ((gamma_sb, gamma), (beta_sb, beta), (bq_sb, bq), (bk_sb, bk)):
                        sp.dma_start(dst[:, :], src.unsqueeze(1)).then_inc(s_const, 16)
                    for dst, src in ((bv_bc, bv), (bo_bc, bo), (br_bc, br)):
                        sp.dma_start(dst[:, :], src.partition_broadcast(128)).then_inc(s_const, 16)
                    for dst, src in ((wq_sb, wq), (wk_sb, wk), (wv_sb, wv), (wo_sb, wo), (wr_sb, wr)):
                        sp.dma_start(dst[:, :], src).then_inc(s_const, 16)

            sp.wait_ge(s_pool_c, 2)
            sp.dma_start(rows_dram[DEAD:DEAD + D, :], pad_row[:, :]).then_inc(s_pad, 16)

            def load_group(par, g):
                for dst, src, parts in ((q_rows, q_dram, Q_PARTS), (k_rows, k_dram, K_PARTS)):
                    for n, part in enumerate(parts):
                        sp.dma_start(dst[par][DH * n:DH * (n + 1), GH * g:GH * (g + 1), 0:L],
                                     src[64 * g:64 * (g + 1), part, :].rearrange("(h j) t -> j h t", j=DH))\
                          .then_inc(s_ld[g], 16)

            def body(i, par):
                if live(i, 1):
                    wait(sp, s_st, STEPS * i if live(i, -1) else 0)
                    load_group(1 - par, 1)
                if live(i, 0):
                    sp.wait_ge(s_free[0], turn_of(i, "MAX1", 0))
                    for n in range(2):
                        sp.dma_start(q_rows[par][KR + n:KR + n + 1, GH:H, 0:L],
                                     max_rows[1][GH * n:GH * (n + 1), :]).then_inc(s_mrow, 16)
                if isinstance(i, int) and i == W_LAST + 2:
                    sp.wait_ge(s_ln2, W_LAST * 3 + 1)
                    sp.dma_start(w_sb[:, :, W1:W1 + HID], w1.rearrange("e p n -> p e n")).then_inc(s_w, 16)
                    for e in range(E):
                        sp.dma_start(w_sb[:, e, W2:W2 + HID].rearrange("p (j n) -> p j n", j=JH),
                                     w2[e].rearrange("(j p) n -> p j n", p=128)).then_inc(s_w, 16)
                    sp.dma_start(w_sb[:, :, B2:B2 + D], b2.partition_broadcast(128)).then_inc(s_w, 16)
                    sp.dma_start(w_sb[:, :, B1:B1 + JH], b1).then_inc(s_w, 16)
                if live(i, 2):
                    wait(sp, s_ld[1], (i + 2) * 192)
                    sp.wait_ge(s_split, (i + 2) * 6 + 3)
                    sp.dma_start(q_dram, q_part[:, :, :]).then_inc(s_qk_w, 16)
                    sp.wait_ge(s_split, (i + 2) * 6 + 6)
                    sp.dma_start(k_dram, k_part[:, :, :]).then_inc(s_qk_w, 16)
                if live(i, 1):
                    sp.wait_ge(s_free[0], turn_of(i, "MAX0", 0))
                    for n in range(2):
                        sp.dma_start(q_rows[1 - par][KR + n:KR + n + 1, 0:GH, 0:L],
                                     max_rows[0][GH * n:GH * (n + 1), :]).then_inc(s_mrow, 16)
                if live(i, 2):
                    if live(i, 0):
                        sp.wait_ge(s_st, i * STEPS + STEPS // 2)
                    sp.wait_ge(s_qk_w, (i + 2) * 32 + 32)
                    load_group(par, 0)

            run_bodies(sp, body)

            pad_regions(sp, range(0, E, 2))
            sp.wait_ge(s_scat, B * NT * 16)
            sp.wait_ge(s_pad, (E + 1) * 16)
            sp.wait_ge(s_tab, TABLES)

            def load_slot(s, n, r):
                if not isinstance(r, int) or r > 0:
                    sp.wait_ge(s_fy, s - (ROUND - 1))
                first = sp.value_load(slot_r_i[0:1, bass.ds(s, 1)], min_val=0, max_val=DEAD)
                sp.dma_start(slot_rows[n][:, :], rows_dram[bass.ds(first, D), :]).then_inc(s_in[n], 16)

            run_slots(sp, 0, load_slot)
            for n in range(ROUND):
                sp.wait_ge(s_out[n], 16 * len(range(n, SLOTS, ROUND)))

        @block.gpsimd
        def _(pool):
            nc.gpsimd.memset(ident[:, :], 0.0)
            nc.gpsimd.memset(identb[:, :], 0.0)
            nc.gpsimd.memset(before[:, :], 1.0)
            nc.gpsimd.memset(valid[:, :, :], 1.0)
            nc.gpsimd.memset(far[:, :], 0.0)
            nc.gpsimd.memset(pad_row[:, :], 0.0).then_inc(s_pool_c, 1)
            pool.wait_ge(s_pool_c, 1)
            for m in (ident, identb):
                nc.gpsimd.affine_select(out=m[:, :], in_=m[:, :], compare_op=ALU.not_equal, fill=1.0, base=0,
                                        pattern=[[-1, 128]], channel_multiplier=1)
            nc.gpsimd.affine_select(out=before[:, :], in_=before[:, :], compare_op=ALU.is_gt, fill=0.0, base=0,
                                    pattern=[[1, 128]], channel_multiplier=-1)
            nc.gpsimd.affine_select(out=valid[:, :, :], in_=valid[:, :, :], compare_op=ALU.is_gt, fill=0.0,
                                    base=L, pattern=[[-D, NT], [0, E]], channel_multiplier=-1)
            nc.gpsimd.affine_select(out=far[:, :], in_=far[:, :], compare_op=ALU.is_gt, fill=float(FAR),
                                    base=L, pattern=[[-D, NT]], channel_multiplier=-1)
            nc.gpsimd.iota(tok_id[:, :], [[D, NT]], base=0, channel_multiplier=1,
                           allow_small_or_imprecise_dtypes=True)
            nc.gpsimd.iota(rank_e[:, :, :], [[0, NT], [-1, E]], base=E, channel_multiplier=0,
                           allow_small_or_imprecise_dtypes=True)
            nc.gpsimd.iota(region[:, :], [[CAP, E]], base=0, channel_multiplier=0,
                           allow_small_or_imprecise_dtypes=True)
            nc.gpsimd.iota(next_row[:, :], [[CAP, E]], base=0, channel_multiplier=0,
                           allow_small_or_imprecise_dtypes=True)
            nc.gpsimd.iota(lane[:, :], [[0, 1]], base=0, channel_multiplier=1,
                           allow_small_or_imprecise_dtypes=True)
            nc.gpsimd.iota(pad_row[:, ID:ID + 1].bitcast(i32), [[0, 1]], base=FAR, channel_multiplier=0)\
              .then_inc(s_pool_c, 1)
            pool.wait_ge(s_vec_c, 1)
            pool.wait_ge(s_tok_st, 2 * B + 2)
            nc.gpsimd.tensor_tensor(bn_rstd[:, :], bn_var[:, :], minus_half[:, 0:1], ALU.pow).then_inc(s_bn_pow, 1)

            def body(i, par):
                if live(i, 2):
                    b = i + 2
                    pool.wait_ge(s_ln, b * 3 + 3)
                    nc.gpsimd.tensor_tensor(rstd[:, :], var_eps[:, :], minus_half[:, :], ALU.pow).then_inc(s_ln_p, 1)
                    if is_body(i, FIRST_BODY):
                        pool.wait_ge(s_ln_p, b * 3 + 2)
                    else:
                        wait_apart(pool, s_ln_p, b * 3 + 1, s_apart_p)
                        norm_rows(nc.gpsimd, lambda t: xn[:, t, :], lambda t: h_cur[:, t, :], mv, rstd, s_ln_p)
                    nc.gpsimd.tensor_tensor(seq[:, bass.ds(b * LP, LP)].rearrange("p (t d) -> p t d", t=NT),
                                            h_cur[:, :, :], bo_bc[:, :].unsqueeze(1).to_broadcast([128, NT, D]),
                                            ALU.add).then_inc(s_ln_p, 1)
                if live(i, -1):
                    r = i - 1
                    pool.wait_ge(s_ln2, r * 3 + 3)
                    nc.gpsimd.tensor_tensor(rstd2[:, :], var_eps2[:, :], minus_half[:, :], ALU.pow)\
                      .then_inc(s_ln2_p, 1)
                    if not is_body(i, LAST_BODY):
                        wait_apart(pool, s_ln2_p, r * 2 + 1, s_apart_p)
                        norm_rows(nc.gpsimd, lambda t: rows[:, t, D:2 * D], lambda t: rows[:, t, 0:D],
                                  mv2, rstd2, s_ln2_p)
                if live(i, 2) and not is_body(i, FIRST_BODY):
                    split(pool, nc.gpsimd, s_apart_p, i, "Q")
                    split(pool, nc.gpsimd, s_apart_p, i, "K")
                if live(i, -1):
                    pool.wait_ge(s_rk, r * 5 + 5)
                    wait_apart(pool, s_rt, r * 10 + 10, s_apart_p)
                    for t in range(NT):
                        pool.indirect_dma_start(
                            out=rows_dram, out_offset=bass.IndirectOffsetOnAxis(ap=pos_i[:, t:t + 1], axis=0),
                            in_=rows[:, t, :], in_offset=None, bounds_check=DEAD - 1, oob_is_err=False)\
                            .then_inc(s_scat, 16)

            run_bodies(pool, body)

            def store_slot(s, n, r):
                wait_apart(pool, s_fy, s + 1, s_apart_p)
                pool.indirect_dma_start(
                    out=out_rows,
                    out_offset=bass.IndirectOffsetOnAxis(ap=slot_id[:, n:n + 1], axis=0),
                    in_=slot_y[n][:, :], in_offset=None, bounds_check=NTOK - 1, oob_is_err=False)\
                    .then_inc(s_out[n], 16)

            run_slots(pool, 0, store_slot)

        @block.scalar
        def _(act):
            act.wait_ge(s_tokw, 16 * 2)
            for n in range(2 * B):
                act.wait_ge(s_tok, n + 1)
                b, half = n // 2, n % 2
                nc.scalar.activation(seq[:, b * LP + half * HALF:b * LP + (half + 1) * HALF],
                                     psum[:, n % 8, 0:HALF], ACT.Relu, bias=tok_b_sb[:, 0:1]).then_inc(s_tok_y, 1)
            act.wait_ge(s_tok_st, 2 * B + 5)
            act.wait_ge(s_vec_c, 1)

            def normed(b, k):
                last = nc.scalar.activation(h_t[:, HALF * k:HALF * (k + 1)], seq[:, bass.ds(b * LP + HALF * k, HALF)],
                                            ACT.Identity, bias=bn_shift[:, 0:1], scale=bn_scale[:, 0:1])
                if k == 1:
                    last.then_inc(s_ht, 1)

            normed(0, 0)
            normed(0, 1)

            def copy_out(i, name, bank, dst):
                act.wait_ge(s_misc, fill(i, name, bank))
                nc.scalar.copy(dst, misc[bank][:, 0:3 * D]).then_inc(s_free[bank], 1)

            def max_out(i, b, g, name):
                act.wait_ge(s_misc, fill(i, name, 0))
                wait(act, s_mrow, (b - 1) * 64 + 32 * (g + 1) if not isinstance(b, int) or b > 0 else 0)
                nc.scalar.copy(max_rows[g][:, :], misc_b[0:2 * GH, 0:L]).then_inc(s_free[0], 1)

            def q_or_k(i, name, bank, k):
                full, part, bias, scale = {"Q": (q_full, q_part, bq4, SCALE), "K": (k_full, k_part, bk_sb, 1.0)}[name]
                dst = (full[:, :] if k == 0 else part[:, 0, :])[:, HALF * bank:HALF * (bank + 1)]
                if k == 0:
                    act.wait_ge(s_misc, fill(i, name, bank))
                    wait(act, s_qk_w, (i + 2) * 32)
                last = nc.scalar.activation(dst, misc[bank][:, 0:HALF], ACT.Identity, bias=bias[:, 0:1], scale=scale)
                if k == 1:
                    last.then_inc(s_free[bank], 1)

            def body(i, par):
                for s in range(STEPS):
                    if live(i, 0):
                        g, qh, kt, h, j = step_of(s)
                        G = s // GH
                        if j == 0:
                            wait(act, s_pv, i * GROUPS + (G - N_P + 1))
                        act.wait_ge(s_st, i * STEPS + (s + 1))
                        nc.scalar.activation(probs[0:kn(kt), G % N_P, j, :], st_bank[s % N_ST][0:kn(kt), 0:HALF],
                                             ACT.Exp).then_inc(s_exp, 1)
                    if s % PASS == OUT_AT:
                        b, p = (i, s // PASS - 1) if s >= PASS else (i - 1, 3)
                        if live(i, 0 if s >= PASS else -1):
                            act.wait_ge(s_pv, b * GROUPS + NT * (p + 1))
                            if p < 2 and live(i, -1):
                                act.wait_ge(s_misc, fill(i, f"OT{p}", 1))
                            nc.scalar.copy(o_un[:, p // 2, p % 2 * HALF:(p % 2 + 1) * HALF], o_bank[:, 0:HALF])\
                              .then_inc(s_o, 1)
                    if s == 3 and live(i, 0):
                        max_out(i, i, 1, "MAX1")
                    if s in (17, 19) and live(i, 2):
                        bank = (s - 17) // 2
                        wait(act, s_ln_p, (i + 2) * 3)
                        copy_out(i, "HTOK", bank, h_cur[:, 3 * bank:3 * (bank + 1), :].rearrange("p t d -> p (t d)"))
                    if s in (31, 33) and live(i, -1):
                        bank = (s - 31) // 2
                        copy_out(i, "MT", bank, merged_t[:, 3 * D * bank:3 * D * (bank + 1)])
                    if s in (41, 43) and live(i, 2):
                        bank = (s - 41) // 2
                        copy_out(i, "XNT", bank, xn_t[:, 3 * D * bank:3 * D * (bank + 1)])
                    if 48 <= s < 52 and live(i, 2):
                        q_or_k(i, "Q", (s - 48) // 2, s % 2)
                    if s == 55 and live(i, 1):
                        max_out(i, i + 1, 0, "MAX0")
                    if 60 <= s < 64 and live(i, 2):
                        q_or_k(i, "K", (s - 60) // 2, s % 2)
                    if s in (65, 67) and live(i, -1):
                        bank = (s - 65) // 2
                        copy_out(i, "XN2T", bank, xn2_t[:, 3 * D * bank:3 * D * (bank + 1)])
                    if s == 83 and live(i, -1):
                        act.wait_ge(s_rt, (i - 1) * 10 + 7)
                        nc.scalar.activation(g_exp[:, :], g_diff[:, :], ACT.Exp).then_inc(s_gate, 1)
                    if s in (25, 27) and live(i, 3):
                        if s == 25:
                            act.wait_ge(s_misc, fill(i, "HTOK", 1))
                        normed(i + 3, s // 27)

            run_bodies(act, body)

            pad_regions(act, range(1, E, 2))

            def relu(s, n):
                act.wait_ge(s_f1, s + 1)
                act.wait_ge(s_fw, s + 1)
                if not isinstance(s, int) or s >= 2:
                    act.wait_ge(s_f2, s - 1)
                for k in range(JH):
                    last = nc.scalar.activation(slot_ht[n % 2][:, D * k:D * (k + 1)],
                                                psum[:, 2 + n % 2, D * k:D * (k + 1)], ACT.Relu,
                                                bias=slot_w[n % N_W][:, B1 + k:B1 + k + 1])
                last.then_inc(s_fr, 1)

            def xt_evac(s, n):
                act.wait_ge(s_fx, s + 1)
                if not isinstance(s, int) or s >= 2:
                    act.wait_ge(s_f1, s - 1)
                nc.scalar.copy(slot_xt[n % 2][:, :], psum[:, n % 2, 0:D]).then_inc(s_fxt, 1)

            def act_turn(s, n, r):
                if not isinstance(s, int) or s + 1 < SLOTS:
                    xt_evac(s + 1, n + 1)
                relu(s, n)

            xt_evac(0, 0)
            run_slots(act, 1, act_turn)

        @block.vector
        def _(dve):
            nc.vector.memset(minus_half[:, :], -0.5)
            nc.vector.memset(ones_b[:, :], 1.0)
            nc.vector.memset(zero_b[:, :], 0.0)
            nc.vector.memset(onehot[:, NT, :], 0.0)
            nc.vector.memset(h_t[:, L:LP], 0.0)
            nc.vector.memset(o_un[:, :, L:LP], 1.0)
            nc.vector.memset(rows[:, :, 2 * D:ROW], 0.0)
            nc.vector.memset(zero_e[:, :], 0.0)
            for n in range(2):
                nc.vector.memset(q_rows[n][0:KR, :, L:LP], 0.0)
                nc.vector.memset(k_rows[n][KR:KM, :, :], 1.0)
                nc.vector.memset(values[n][:, :, :, DH:32], 1.0)
            dve.wait_ge(s_const, 16 * 12)
            nc.vector.tensor_scalar(bq4[:, :], bq_sb[:, :], SCALE, None, ALU.mult).then_inc(s_vec_c, 1)

            for n in range(2 * B):
                dve.wait_ge(s_tok_y, n + 1)
                b, half = n // 2, n % 2
                nc.vector.bn_stats(bn_stats[:, n, :],
                                   seq[:, b * LP + half * HALF:b * LP + (half + 1) * HALF]).then_inc(s_tok_st, 1)
            dve.wait_ge(s_tok_st, 2 * B)
            nc.vector.bn_aggr(bn_mv[:, :], bn_stats[:, :, :]).then_inc(s_tok_st, 1)
            dve.wait_ge(s_tok_st, 2 * B + 1)
            nc.vector.tensor_scalar(bn_var[:, :], bn_mv[:, 1:2], EPS, None, ALU.add).then_inc(s_tok_st, 1)
            dve.wait_ge(s_bn_pow, 1)
            nc.vector.tensor_tensor(bn_scale[:, :], bn_rstd[:, :], gamma_sb[:, :], ALU.mult).then_inc(s_tok_st, 1)
            dve.wait_ge(s_tok_st, 2 * B + 3)
            nc.vector.tensor_tensor(bn_ms[:, :], bn_mv[:, 0:1], bn_scale[:, :], ALU.mult).then_inc(s_tok_st, 1)
            dve.wait_ge(s_tok_st, 2 * B + 4)
            nc.vector.tensor_tensor(bn_shift[:, :], beta_sb[:, :], bn_ms[:, :], ALU.subtract).then_inc(s_tok_st, 1)
            dve.wait_ge(s_pool_c, 2)

            def layer_stats(b, k, tiles_of, st, mean_var, out_var, counter):
                if k < 3:
                    for t in (2 * k, 2 * k + 1):
                        last = nc.vector.bn_stats(st[:, t, :], tiles_of[:, t, 0:D])
                    if k == 2:
                        last.then_inc(counter, 1)
                elif k < 5:
                    if k == 3:
                        wait_apart(dve, counter, b * 3 + 1, s_apart_v)
                    for t in range(3 * (k - 3), 3 * (k - 2)):
                        last = nc.vector.bn_aggr(mean_var[:, t, :], st[:, t, :])
                    if k == 4:
                        last.then_inc(counter, 1)
                else:
                    dve.wait_ge(counter, b * 3 + 2)
                    nc.vector.tensor_scalar(out_var[:, :], mean_var[:, :, 1], EPS, None, ALU.add)\
                      .then_inc(counter, 1)

            def maxima(b, g):
                k = 3 * g
                dve.wait_ge(s_red, b * STEPS + STEPS // 2 * (g + 1))
                nc.vector.tensor_reduce(neg_max[:, 24 * g:24 * (g + 1)],
                                        half_max[:, 48 * g:48 * (g + 1)].rearrange("p (n a) -> p n a", a=2),
                                        AX.X, ALU.max, negate=True).then_inc(s_max, 1)
                dve.wait_ge(s_max, b * 6 + (k + 1))
                full = neg_max[:, 24 * g:24 * (g + 1)].rearrange("p (h t) -> p t h", h=GH)
                nc.vector.tensor_copy(max_parts[:, g, :, 0, :], full).then_inc(s_max, 1)
                dve.wait_ge(s_max, b * 6 + (k + 2))
                nc.vector.tensor_tensor(max_parts[:, g, :, 1, :], full, max_parts[:, g, :, 0, :], ALU.subtract)\
                  .then_inc(s_max, 1)

            def normalise(i, r, c, bank, k):
                o = misc[bank][:, 0:3 * D].rearrange("p (n c) -> p n c", c=32)
                n = 2 * c + bank
                if k == 0:
                    dve.wait_ge(s_misc, fill(i, f"OT{c}", bank))
                    nc.vector.reciprocal(r_den[:, n, :], o[:, :, DH]).then_inc(s_den, 1)
                else:
                    dve.wait_ge(s_den, r * 4 + (n + 1))
                    nc.vector.tensor_tensor(
                        merged[:, :, :].rearrange("p t (h d) -> p (t h) d", h=H)[:, 12 * n:12 * (n + 1), :],
                        o[:, :, 0:DH], r_den[:, n, :].unsqueeze(2).to_broadcast([128, NT // 2 * GH, DH]), ALU.mult)\
                        .then_inc(s_free[bank], 1)

            def bias_values(i, par, k):
                dve.wait_ge(s_misc, fill(i, "V", k))
                nc.vector.tensor_tensor(
                    values[1 - par][:, 3 * k:3 * (k + 1), :, 0:DH],
                    misc[k][:, 0:3 * D].rearrange("p (t h d) -> p t h d", t=3, h=H),
                    bv_bc[:, :].rearrange("p (h d) -> p h d", h=H).unsqueeze(1).to_broadcast([128, 3, H, DH]), ALU.add)\
                    .then_inc(s_free[k], 1)

            def residual(i, r, k):
                dve.wait_ge(s_misc, fill(i, "PROJ", k))
                if k == 0:
                    dve.wait_ge(s_ln_p, r * 3 + 3)
                    wait(dve, s_scat, r * (NT * 16))
                nc.vector.tensor_tensor(
                    rows[:, 3 * k:3 * (k + 1), 0:D], misc[k][:, 0:3 * D].rearrange("p (t d) -> p t d", t=3),
                    seq[:, bass.ds(r * LP + 3 * D * k, 3 * D)].rearrange("p (t d) -> p t d", t=3), ALU.add)\
                    .then_inc(s_free[k], 1)

            def per(a):
                return a[:, :].unsqueeze(2).to_broadcast([128, NT, E])

            def router(i, r, k):
                if k == 0:
                    dve.wait_ge(s_misc, fill(i, "LOGIT", 0))
                    nc.vector.tensor_tensor(logits[:, :, :], misc[0][:, 0:NT * E].rearrange("p (t e) -> p t e", t=NT),
                                            br_bc[:, :].unsqueeze(1).to_broadcast([128, NT, E]), ALU.add)\
                      .then_inc(s_free[0], 1)
                elif k == 1:
                    dve.wait_ge(s_free[0], turn_of(i, "LOGIT", 0))
                    nc.vector.reduce_max(top[:, :], logits[:, :, :], AX.X).then_inc(s_rt, 1)
                elif k == 2:
                    dve.wait_ge(s_rt, r * 10 + 1)
                    nc.vector.tensor_tensor(scored[:, :, :], logits[:, :, :], per(top), ALU.is_equal)\
                      .then_inc(s_rt, 1)
                elif k == 3:
                    dve.wait_ge(s_rt, r * 10 + 2)
                    nc.vector.tensor_tensor(scored2[:, :, :], scored[:, :, :], rank_e[:, :, :], ALU.mult)\
                      .then_inc(s_rt, 1)
                elif k == 4:
                    dve.wait_ge(s_rt, r * 10 + 3)
                    nc.vector.reduce_max(best[:, :], scored2[:, :, :], AX.X).then_inc(s_rt, 1)
                elif k == 5:
                    dve.wait_ge(s_rt, r * 10 + 4)
                    nc.vector.tensor_tensor(picked[:, :, :], rank_e[:, :, :], per(best), ALU.is_equal)\
                      .then_inc(s_rt, 1)
                elif k == 6:
                    dve.wait_ge(s_rt, r * 10 + 5)
                    nc.vector.tensor_tensor(onehot[:, 0:NT, :], picked[:, :, :], valid[:, :, :], ALU.mult)\
                      .then_inc(s_rt, 1)
                elif k == 7:
                    nc.vector.tensor_tensor(g_diff[:, :], top[:, :], top[:, :], ALU.subtract).then_inc(s_rt, 1)
                elif k == 8:
                    dve.wait_ge(s_gate, r + 1)
                    nc.vector.reciprocal(g_inv[:, :], g_exp[:, :]).then_inc(s_rt, 1)
                else:
                    dve.wait_ge(s_rt, r * 10 + 8)
                    nc.vector.tensor_tensor(rows[:, :, GATE], g_exp[:, :], g_inv[:, :], ALU.mult).then_inc(s_rt, 1)

            def ranks(i, r, k):
                if k == 0:
                    dve.wait_ge(s_misc, fill(i, "RANK", 0))
                    nc.vector.tensor_tensor(place[:, :, :], misc[0][:, 0:NT * E].rearrange("p (t e) -> p t e", t=NT),
                                            next_row[:, :].unsqueeze(1).to_broadcast([128, NT, E]), ALU.add)\
                      .then_inc(s_rk, 1)
                elif k == 1:
                    dve.wait_ge(s_rk, r * 5 + 1)
                    nc.vector.tensor_tensor(next_row[:, :], misc[0][:, NT * E:(NT + 1) * E], next_row[:, :], ALU.add)\
                      .then_inc(s_free[0], 1)
                    nc.vector.tensor_copy(rows[:, :, ID].bitcast(i32), tok_id[:, :]).then_inc(s_rk, 1)
                elif k == 2:
                    nc.vector.tensor_tensor(place1[:, :, :], place[:, :, :], onehot[:, 0:NT, :], ALU.mult)\
                      .then_inc(s_rk, 1)
                elif k == 3:
                    dve.wait_ge(s_rk, r * 5 + 3)
                    nc.vector.reduce_sum(pos[:, :], place1[:, :, :], AX.X).then_inc(s_rk, 1)
                elif k == 4:
                    dve.wait_ge(s_rk, r * 5 + 4)
                    nc.vector.tensor_tensor(pos_i[:, :], pos[:, :], far[:, :], ALU.add).then_inc(s_rk, 1)
                else:
                    dve.wait_ge(s_rk, r * 5 + 2)
                    nc.vector.tensor_scalar(tok_id[:, :], tok_id[:, :], float(L), None, ALU.add).then_inc(s_rt, 1)

            def body(i, par):
                for s in range(STEPS):
                    if live(i, 1):
                        dve.wait_ge(s_mx, (i + 1) * STEPS + (s + 1))
                        nc.vector.tensor_reduce(half_max[:, s:s + 1], mx_bank[s % N_MX][:, 0:HALF], AX.X, ALU.max)\
                          .then_inc(s_red, 1)
                        if s % 48 == 47:
                            maxima(i + 1, s // 48)
                    if 9 <= s < 17 and live(i, -1):
                        normalise(i, i - 1, (s - 9) // 4, (s - 9) % 4 // 2, (s - 9) % 2)
                    if 20 <= s < 26 and live(i, 2):
                        if s == 20:
                            for bank in range(2):
                                dve.wait_ge(s_free[bank], turn_of(i, "HTOK", bank))
                        layer_stats(i + 2, s - 20, h_cur, stats, mv, var_eps, s_ln)
                    if s == 26 and is_body(i, FIRST_BODY):
                        dve.wait_ge(s_ln_p, 1)
                        norm_rows(nc.vector, lambda t: xn[:, t, :], lambda t: h_cur[:, t, :], mv, rstd, s_ln_p)
                    if s == 60 and is_body(i, FIRST_BODY):
                        split(dve, nc.vector, s_apart_v, i, "Q")
                        split(dve, nc.vector, s_apart_v, i, "K")
                    if s in (26, 27) and live(i, 1):
                        bias_values(i, par, s - 26)
                    if s in (36, 39) and live(i, -1):
                        residual(i, i - 1, s // 39)
                    if 40 <= s < 46 and live(i, -1):
                        if s == 40:
                            for bank in range(2):
                                dve.wait_ge(s_free[bank], turn_of(i, "PROJ", bank))
                        layer_stats(i - 1, s - 40, rows, stats2, mv2, var_eps2, s_ln2)
                    if s == 46 and is_body(i, LAST_BODY):
                        dve.wait_ge(s_ln2_p, (B - 1) * 2 + 1)
                        norm_rows(nc.vector, lambda t: rows[:, t, D:2 * D], lambda t: rows[:, t, 0:D],
                                  mv2, rstd2, s_ln2_p)
                    if 74 <= s < 82 and live(i, -1):
                        router(i, i - 1, s - 74)
                    if 85 <= s < 87 and live(i, -1):
                        router(i, i - 1, s - 77)
                    if 87 <= s < 93 and live(i, -1):
                        ranks(i, i - 1, s - 87)

            run_bodies(dve, body)

            nc.vector.tensor_copy(pad_i[:, :], next_row[0:1, :]).then_inc(s_tab, 1)
            nc.vector.tensor_tensor(count[:, :], next_row[:, :], region[:, :], ALU.subtract).then_inc(s_tab, 1)
            dve.wait_ge(s_tab, 2)
            nc.vector.tensor_scalar(tiles_f[:, :], count[:, :], 1.0 / D, (D - 1) / D - (D - 1) / (2 * D),
                                    ALU.mult, ALU.add).then_inc(s_tab, 1)
            dve.wait_ge(s_tab, 3)
            nc.vector.tensor_copy(tiles_i[:, :], tiles_f[:, :]).then_inc(s_tab, 1)
            dve.wait_ge(s_tab, 4)
            nc.vector.tensor_copy(tiles[:, :], tiles_i[:, :]).then_inc(s_tab, 1)
            dve.wait_ge(s_tab, 5)
            nc.vector.tensor_tensor_scan(cum[:, :], tiles[:, :], zero_e[:, :], 0.0, ALU.add, ALU.add)
            nc.vector.tensor_scalar(skip_e[:, :], tiles[:, :], -float(D), float(CAP), ALU.mult, ALU.add)\
              .then_inc(s_tab, 1)
            dve.wait_ge(s_tab, 6)
            nc.vector.tensor_scalar(beyond[:, :], cum[:, :], lane[:, 0:1], None, ALU.is_le).then_inc(s_tab, 1)
            dve.wait_ge(s_tab, 7)
            nc.vector.tensor_tensor(beyond_w[:, :], beyond[:, :], skip_e[:, :], ALU.mult)
            nc.vector.reduce_sum(slot_e[:, :], beyond[:, :], AX.X).then_inc(s_tab, 1)
            dve.wait_ge(s_tab, 8)
            nc.vector.reduce_sum(slot_r0[:, :], beyond_w[:, :], AX.X).then_inc(s_tab, 1)
            dve.wait_ge(s_tab, 9)
            nc.vector.scalar_tensor_tensor(slot_r[:, :], lane[:, :], float(D), slot_r0[:, :], ALU.mult, ALU.add)\
              .then_inc(s_tab, 1)
            dve.wait_ge(s_tab_t, 1)
            nc.vector.tensor_scalar(slot_e_i[:, :], misc[0][0:1, 0:D], float(E - 1), None, ALU.min)
            nc.vector.tensor_scalar(slot_r_i[:, :], misc[0][0:1, D:2 * D], float(DEAD), None, ALU.min)\
              .then_inc(s_tab, 1)
            dve.wait_ge(s_tab, TABLES)
            dve.wait_ge(s_w, 16 * (E + 3))

            def expert_of(s):
                return dve.value_load(slot_e_i[0:1, bass.ds(s, 1)], min_val=0, max_val=E - 1)

            def weights(e, n):
                nc.vector.tensor_copy(slot_w[n % N_W].unsqueeze(1), w_sb[:, bass.ds(e, 1), :]).then_inc(s_fw, 1)

            def dve_turn(s, n, r):
                more = not isinstance(s, int) or s + N_W < SLOTS
                e = expert_of(s + N_W) if more else None
                if not isinstance(r, int) or r > 0:
                    dve.wait_ge(s_out[n], r * 16)
                dve.wait_ge(s_in[n], r * 16 + 16)
                nc.vector.tensor_copy(slot_id[:, n:n + 1], slot_rows[n][:, ID:ID + 1].bitcast(i32))
                dve.wait_ge(s_f2, s + 1)
                nc.vector.tensor_tensor(slot_y[n][:, :], psum[:, 5 + n % 3, 0:D], slot_w[n % N_W][:, B2:B2 + D],
                                        ALU.add).then_inc(s_fb, 1)
                dve.wait_ge(s_fb, s + 1)
                if more:
                    weights(e, n)
                nc.vector.scalar_tensor_tensor(slot_y[n][:, :], slot_y[n][:, :], slot_rows[n][:, GATE:GATE + 1],
                                               slot_rows[n][:, 0:D], ALU.mult, ALU.add).then_inc(s_fy, 1)

            for s in range(N_W):
                weights(expert_of(s), s)
            run_slots(dve, N_W, dve_turn)

        @block.tensor
        def _(pe):
            pe.wait_ge(s_tokw, 16 * 2)
            for n in range(2 * B):
                c, b, half = n // (2 * CH), n // 2, n % 2
                if n % (2 * CH) == 0:
                    pe.wait_ge(s_patch[c % N_P], 16 * CONTEXT * (c // N_P + 1))
                if n >= 8:
                    pe.wait_ge(s_tok_y, n - 7)
                nc.tensor.matmul(psum[:, n % 8, 0:HALF], tok_w_sb[:, :],
                                 patches[:, c % N_P, b % CH, half * HALF:(half + 1) * HALF],
                                 start=True, stop=True).then_inc(s_tok, 1)
            pe.wait_ge(s_tok_y, 2 * B)
            pe.wait_ge(s_pool_c, 2)
            pe.wait_ge(s_vec_c, 1)
            pe.wait_ge(s_const, 16 * 12)

            def transposes(bank, src):
                for n in range(3):
                    last = nc.tensor.transpose(misc[bank][:, D * n:D * (n + 1)], src(3 * bank + n), ident[:, :])
                return last

            def task(i, par, name, bank, k, pieces):
                if k == 0:
                    wait(pe, s_free[bank], turn_of(i, name, bank) - 1)
                if name == "V":
                    t = 3 * bank + k
                    last = nc.tensor.matmul(misc[bank][:, D * k:D * (k + 1)], xn_t[:, D * t:D * (t + 1)], wv_sb[:, :],
                                            start=True, stop=True)
                elif name in ("MAX0", "MAX1"):
                    g = int(name[3])
                    pe.wait_ge(s_max, (i + (1 - g)) * 6 + 3 * (g + 1))
                    for t in range(NT):
                        last = nc.tensor.transpose(misc_b[0:2 * GH, D * t:D * (t + 1)],
                                                   max_parts[:, g, t, :, :].rearrange("p a h -> p (a h)"), identb[:, :])
                elif name in ("OT0", "OT1"):
                    pe.wait_ge(s_o, (i - 1) * 4 + 4)
                    t0 = 3 * int(name[2])
                    last = transposes(bank, lambda n: o_un[:, n % 2, D * (t0 + n // 2):D * (t0 + n // 2 + 1)])
                elif name == "HTOK":
                    pe.wait_ge(s_ht, (i + 2) + 1)
                    last = transposes(bank, lambda t: h_t[:, D * t:D * (t + 1)])
                elif name == "MT":
                    pe.wait_ge(s_free[1], turn_of(i, f"OT{bank}", 1))
                    last = transposes(bank, lambda t: merged[:, t, :])
                elif name == "XNT":
                    pe.wait_ge(s_ln_p, (i + 2) * 3 + 2)
                    last = transposes(bank, lambda t: xn[:, t, :])
                elif name == "PROJ":
                    t = 3 * bank + k
                    last = nc.tensor.matmul(misc[bank][:, D * k:D * (k + 1)], merged_t[:, D * t:D * (t + 1)],
                                            wo_sb[:, :], start=True, stop=True)
                elif name in ("Q", "K"):
                    first, n = (0, HALF // 2) if k == 0 else (HALF // 2, HALF - HALF // 2)
                    last = nc.tensor.matmul(misc[bank][:, first:first + n], (wq_sb if name == "Q" else wk_sb)[:, :],
                                            xn_t[:, bank * HALF + first:bank * HALF + first + n],
                                            start=True, stop=True)
                elif name == "XN2T":
                    pe.wait_ge(s_ln2_p, (i - 1) * 2 + 2)
                    last = transposes(bank, lambda t: rows[:, t, D:2 * D])
                elif name == "LOGIT":
                    if k == 0:
                        pe.wait_ge(s_free[1], turn_of(i, "XN2T", 1))
                    for t in range(3 * k, 3 * (k + 1)):
                        last = nc.tensor.matmul(misc[0][:, E * t:E * (t + 1)], xn2_t[:, D * t:D * (t + 1)],
                                                wr_sb[:, :], start=True, stop=True)
                else:
                    pe.wait_ge(s_rt, (i - 1) * 10 + 6)
                    nc.tensor.matmul(misc[0][:, 0:(NT + 1) * E], before[:, :],
                                     onehot[:, :, :].rearrange("p t e -> p (t e)"), start=True, stop=False)
                    for t in range(NT):
                        nc.tensor.matmul(misc[0][:, E * (t + 1):(NT + 1) * E].rearrange("p (t e) -> p t e", e=E),
                                         ones_b[:, :], onehot[:, t:t + 1, :].to_broadcast([128, NT - t, E]),
                                         start=False, stop=False)
                    last = nc.tensor.matmul(misc[0][:, 0:(NT + 1) * E], ones_b[:, :], zero_b[:, :],
                                            start=False, stop=True)
                if k == pieces - 1:
                    last.then_inc(s_misc, 1)

            def weigh(b, par, G, k):
                p, kt = G // NT, G % NT
                first = HALF * k // PARTS
                n = HALF * (k + 1) // PARTS - first
                if k == 0:
                    pe.wait_ge(s_exp, b * STEPS + GH * (G + 1))
                    if kt == 0:
                        wait(pe, s_o, b * 4 + p)
                for j in range(GH):
                    last = nc.tensor.matmul(o_bank[32 * j:32 * (j + 1), first:first + n],
                                            values[par][0:kn(kt), kt, GH * (p // 2) + j, :],
                                            probs[0:kn(kt), G % N_P, j, first:first + n],
                                            start=kt == 0 and k == 0, stop=kt == NT - 1, skip_group_check=True)
                if k == PARTS - 1:
                    last.then_inc(s_pv, 1)

            def body(i, par):
                for s in range(STEPS):
                    if live(i, 0):
                        g, qh, kt, h, j = step_of(s)
                        if s % 48 == 0:
                            pe.wait_ge(s_mrow, i * 64 + 32 * (g + 1))
                        wait(pe, s_exp, i * STEPS + (s + 1 - N_ST))
                        nc.tensor.matmul(st_bank[s % N_ST][0:kn(kt), 0:HALF],
                                         k_rows[par][0:KM, h, D * kt:D * kt + kn(kt)],
                                         q_rows[par][0:KM, h, qh * HALF:(qh + 1) * HALF],
                                         start=True, stop=True).then_inc(s_st, 1)
                    if live(i, 1):
                        b, h, t, half = i + 1, s // 12, s % 12 // 2, s % 2
                        if s % 48 == 0:
                            pe.wait_ge(s_ld[s // 48], b * 192 + 192)
                        wait(pe, s_red, b * STEPS + (s + 1 - N_MX))
                        nc.tensor.matmul(mx_bank[s % N_MX][:, 0:HALF], q_rows[1 - par][0:KR, h, D * t:D * (t + 1)],
                                         k_rows[1 - par][0:KR, h, half * HALF:(half + 1) * HALF],
                                         start=True, stop=True).then_inc(s_mx, 1)
                    for n, after in enumerate(WEIGH_AT):
                        p = (s - after) // PASS
                        if (s - after) % PASS == 0 and live(i, 0 if p >= 0 else -1):
                            weigh(i if p >= 0 else i - 1, par if p >= 0 else 1 - par, p % 4 * NT + n // PARTS, n % PARTS)
                    for name, *banks in TASKS:
                        for bank, at in enumerate(banks):
                            if s in at and live(i, STAGE[name]):
                                task(i, par, name, bank, at.index(s), len(at))

            run_bodies(pe, body)

            pe.wait_ge(s_tab, 10)
            nc.tensor.transpose(misc[0][0:1, 0:D], slot_e[:, :], ident[:, :])
            nc.tensor.transpose(misc[0][0:1, D:2 * D], slot_r[:, :], ident[:, :]).then_inc(s_tab_t, 1)

            def x_t_slot(s, n, r):
                pe.wait_ge(s_in[n], r * 16 + 16)
                if not isinstance(s, int) or s >= 2:
                    pe.wait_ge(s_fxt, s - 1)
                nc.tensor.transpose(psum[:, n % 2, 0:D], slot_rows[n][:, D:2 * D], ident[:, :]).then_inc(s_fx, 1)

            def layer1(s, n):
                pe.wait_ge(s_fw, s + 1)
                pe.wait_ge(s_fxt, s + 1)
                if not isinstance(s, int) or s >= 2:
                    pe.wait_ge(s_fr, s - 1)
                for k in range(JH):
                    last = nc.tensor.matmul(psum[:, 2 + n % 2, D * k:D * (k + 1)],
                                            slot_w[n % N_W][:, W1 + D * k:W1 + D * (k + 1)], slot_xt[n % 2][:, :],
                                            start=True, stop=True)
                last.then_inc(s_f1, 1)

            def layer2(s, n):
                pe.wait_ge(s_fr, s + 1)
                if not isinstance(s, int) or s >= 3:
                    pe.wait_ge(s_fb, s - 2)
                for k in range(JH):
                    last = nc.tensor.matmul(psum[:, 5 + n % 3, 0:D], slot_ht[n % 2][:, D * k:D * (k + 1)],
                                            slot_w[n % N_W][:, W2 + D * k:W2 + D * (k + 1)],
                                            start=k == 0, stop=k == JH - 1)
                last.then_inc(s_f2, 1)

            def pe_turn(s, n, r):
                if not isinstance(s, int) or s + 1 < SLOTS:
                    layer1(s + 1, n + 1)
                if not isinstance(s, int) or s + 2 < SLOTS:
                    x_t_slot(*later(s, n, r, 2))
                layer2(s, n)

            x_t_slot(0, 0, 0)
            layer1(0, 0)
            x_t_slot(1, 1, 0)
            run_slots(pe, 2, pe_turn)


def kernel(**inputs):
    import numpy as np
    import concourse.bacc as bacc
    from concourse.bass_utils import run_bass_kernel_spmd

    def a(name):
        return np.asarray(inputs[name])

    b1 = a("L0_ffn_b1")
    channels, taps = inputs["L0_tok_W"].shape
    arrays = {
        "x_t": a("x").transpose(2, 0, 1),
        "tok_w": a("L0_tok_W").T, "tok_b": a("L0_tok_b"), "gamma": a("L0_tok_gamma"), "beta": a("L0_tok_beta"),
        "wq": a("L0_attn_Wq").T, "bq": a("L0_attn_bq"), "wk": a("L0_attn_Wk").T, "bk": a("L0_attn_bk"),
        "wv": a("L0_attn_Wv").T, "bv": a("L0_attn_bv"), "wo": a("L0_attn_Wo").T, "bo": a("L0_attn_bo"),
        "wr": a("L0_ffn_Wr"), "br": a("L0_ffn_br"), "w1": a("L0_ffn_W1"), "b1": b1.reshape(b1.shape[0], -1, channels).transpose(2, 0, 1),
        "w2": a("L0_ffn_W2"), "b2": a("L0_ffn_b2"),
    }
    arrays = {f"in_{n}_dram": np.ascontiguousarray(v) for n, v in arrays.items()}
    nc = bacc.Bacc("TRN2", target_bir_lowering=False, num_devices=1)
    args = [nc.dram_tensor(n, v.shape, mybir.dt.from_np(v.dtype), kind="ExternalInput").ap()
            for n, v in arrays.items()]
    b, frames, feat = inputs["x"].shape
    shape = (b, frames - taps // feat + 1, channels)
    args.append(nc.dram_tensor("out_dram", shape, mybir.dt.float32, kind="ExternalOutput").ap())
    audio_tower(nc, *args)
    return run_bass_kernel_spmd(nc, [arrays], core_ids=[0]).results[0]["out_dram"]
```
